# Optimizing a Trainium2 kernel written in Bass

```python
import numpy as np
import jax
import jax.numpy as jnp

def _softmax(x, axis=-1):
    return jax.nn.softmax(x, axis=axis)

def _gelu(x):
    return jax.nn.gelu(x, approximate=True)

def _silu(x):
    return jax.nn.silu(x)

def _sigmoid(x):
    return jax.nn.sigmoid(x)

def _layernorm(x, axis=-1, eps=1e-05):
    m = jnp.mean(x, axis=axis, keepdims=True)
    v = jnp.var(x, axis=axis, keepdims=True)
    return (x - m) / jnp.sqrt(v + eps)

def _scatter_add(tgt, idx, src, axis=0):
    return tgt.at[idx].add(src)

def _segment_sum(src, seg, n):
    return jax.ops.segment_sum(src, seg, n)
kernel_name = 'mk_adaln_d1_jaxref_r8_812131'

def setup_inputs(seed: int=0):
    np.random.seed(seed)
    _w = jnp.asarray

    def _L0_attn_setup():
        import jax, jax.numpy as jnp
        import numpy as np
        DIM = 128
        HEADS = 16
        HEAD_DIM = DIM // HEADS

        def apply_rope(x):
            B, S, H, D = x.shape
            half = D // 2
            freqs = 1.0 / 10000.0 ** (jnp.arange(half, dtype=jnp.float32) / half)
            pos = jnp.arange(S, dtype=jnp.float32)
            angles = pos[:, None] * freqs[None, :]
            sin = jnp.sin(angles)[None, :, None, :]
            cos = jnp.cos(angles)[None, :, None, :]
            x1, x2 = (x[..., :half], x[..., half:])
            return jnp.concatenate([x1 * cos - x2 * sin, x1 * sin + x2 * cos], axis=-1)
        key = jax.random.key(seed)
        ks = jax.random.split(key, 5)
        x = jax.random.normal(ks[0], (2, 256, DIM), dtype=jnp.float32)
        s = 1.0 / np.sqrt(DIM)
        qkv_w = jax.random.uniform(ks[1], (3 * DIM, DIM), minval=-s, maxval=s, dtype=jnp.float32)
        qkv_b = jax.random.uniform(ks[2], (3 * DIM,), minval=-s, maxval=s, dtype=jnp.float32)
        proj_w = jax.random.uniform(ks[3], (DIM, DIM), minval=-s, maxval=s, dtype=jnp.float32)
        proj_b = jax.random.uniform(ks[4], (DIM,), minval=-s, maxval=s, dtype=jnp.float32)
        return {'x': x, 'qkv_w': qkv_w, 'qkv_b': qkv_b, 'proj_w': proj_w, 'proj_b': proj_b}
    _L0_attn_in = _L0_attn_setup()

    def _L0_ffn_setup():
        import jax, jax.numpy as jnp
        import numpy as np
        NUM_EXPERTS = 160
        TOP_K = 8
        ROUTED_SCALE = 2.5
        HIDDEN = 128
        INTER = 64
        key = jax.random.key(seed)
        ks = jax.random.split(key, 7)
        B, S = (1, 256)
        return {'hidden_states': jax.random.normal(ks[0], (B, S, HIDDEN), dtype=jnp.float32), 'router_w': jax.random.normal(ks[1], (NUM_EXPERTS, HIDDEN), dtype=jnp.float32) * 0.02, 'expert_bias': jnp.zeros((NUM_EXPERTS,), dtype=jnp.float32), 'w_gate': jax.random.normal(ks[2], (NUM_EXPERTS, INTER, HIDDEN), dtype=jnp.float32) * 0.02, 'w_down': jax.random.normal(ks[3], (NUM_EXPERTS, HIDDEN, INTER), dtype=jnp.float32) * 0.02, 'w_gate_shared': jax.random.normal(ks[4], (INTER, HIDDEN), dtype=jnp.float32) * 0.02, 'w_down_shared': jax.random.normal(ks[5], (HIDDEN, INTER), dtype=jnp.float32) * 0.02}
    _L0_ffn_in = _L0_ffn_setup()
    _L0_c = _w((lambda *s: np.random.randn(*s).astype(np.float32) * 0.05)(16, 128))
    _L0_wmod = _w((lambda *s: np.random.randn(*s).astype(np.float32) * 0.05)(128, 6 * 128) * 128 ** (-0.5))
    _d = {'L0_attn_x': _L0_attn_in['x'], 'L0_attn_qkv_w': _L0_attn_in['qkv_w'], 'L0_attn_qkv_b': _L0_attn_in['qkv_b'], 'L0_attn_proj_w': _L0_attn_in['proj_w'], 'L0_attn_proj_b': _L0_attn_in['proj_b'], 'L0_ffn_router_w': _L0_ffn_in['router_w'], 'L0_ffn_expert_bias': _L0_ffn_in['expert_bias'], 'L0_ffn_w_gate': _L0_ffn_in['w_gate'], 'L0_ffn_w_down': _L0_ffn_in['w_down'], 'L0_ffn_w_gate_shared': _L0_ffn_in['w_gate_shared'], 'L0_ffn_w_down_shared': _L0_ffn_in['w_down_shared'], 'L0_c': _L0_c, 'L0_wmod': _L0_wmod}
    _x0 = _d['L0_attn_x']
    _d['L0_attn_x'] = jax.random.normal(jax.random.fold_in(jax.random.key(seed), 1), (16, 512, 128), dtype=_x0.dtype)
    del _x0
    return _d

def reference(L0_attn_x, L0_attn_qkv_w, L0_attn_qkv_b, L0_attn_proj_w, L0_attn_proj_b, L0_ffn_router_w, L0_ffn_expert_bias, L0_ffn_w_gate, L0_ffn_w_down, L0_ffn_w_gate_shared, L0_ffn_w_down_shared, L0_c, L0_wmod):

    def _L0_attn_ref(x, qkv_w, qkv_b, proj_w, proj_b):
        import jax, jax.numpy as jnp
        import numpy as np
        DIM = 128
        HEADS = 16
        HEAD_DIM = DIM // HEADS

        def apply_rope(x):
            B, S, H, D = x.shape
            half = D // 2
            freqs = 1.0 / 10000.0 ** (jnp.arange(half, dtype=jnp.float32) / half)
            pos = jnp.arange(S, dtype=jnp.float32)
            angles = pos[:, None] * freqs[None, :]
            sin = jnp.sin(angles)[None, :, None, :]
            cos = jnp.cos(angles)[None, :, None, :]
            x1, x2 = (x[..., :half], x[..., half:])
            return jnp.concatenate([x1 * cos - x2 * sin, x1 * sin + x2 * cos], axis=-1)
        B, S, D = x.shape
        qkv = x @ qkv_w.T + qkv_b
        q, k, v = jnp.split(qkv, 3, axis=-1)
        q = q.reshape(B, S, HEADS, HEAD_DIM)
        k = k.reshape(B, S, HEADS, HEAD_DIM)
        v = v.reshape(B, S, HEADS, HEAD_DIM)
        q = apply_rope(q)
        k = apply_rope(k)
        scale = 1.0 / np.sqrt(HEAD_DIM)
        attn = jnp.einsum('bqhd,bkhd->bhqk', q, k) * scale
        mask = jnp.triu(jnp.ones((S, S), dtype=bool), k=1)
        attn = jnp.where(mask[None, None], -1000000000.0, attn)
        attn = jax.nn.softmax(attn, axis=-1)
        out = jnp.einsum('bhqk,bkhd->bqhd', attn, v).reshape(B, S, D)
        return out @ proj_w.T + proj_b

    def _L0_ffn_ref(hidden_states, router_w, expert_bias, w_gate, w_down, w_gate_shared, w_down_shared):
        import jax, jax.numpy as jnp
        import numpy as np
        NUM_EXPERTS = 160
        TOP_K = 8
        ROUTED_SCALE = 2.5
        HIDDEN = 128
        INTER = 64
        B, S, H = hidden_states.shape
        x = hidden_states.reshape(-1, H)
        T = x.shape[0]
        logits = x @ router_w.T + expert_bias[None, :]
        probs = jax.nn.sigmoid(logits)
        top_w, top_idx = jax.lax.top_k(probs, TOP_K)
        top_w = top_w / (jnp.sum(top_w, axis=-1, keepdims=True) + 1e-09)
        top_w = top_w * ROUTED_SCALE
        combine = jnp.zeros((T, NUM_EXPERTS), dtype=x.dtype)
        combine = combine.at[jnp.arange(T)[:, None], top_idx].set(top_w)
        h1 = jax.nn.silu(jnp.einsum('th,eih->eti', x, w_gate))
        h1w = h1 * combine.T[:, :, None]
        routed = jnp.einsum('eti,ehi->th', h1w, w_down)
        shared = jax.nn.silu(x @ w_gate_shared.T) @ w_down_shared.T
        return (routed + shared).reshape(B, S, H)
    x = L0_attn_x
    mod = (_silu(L0_c) @ L0_wmod).reshape(L0_c.shape[0], 6, 1, -1)
    sa, ca, ga, sb, cb, gb = (mod[:, 0], mod[:, 1], mod[:, 2], mod[:, 3], mod[:, 4], mod[:, 5])
    ga = (2 * (ga >= 0) - 1) * jnp.maximum(jnp.abs(ga), 0.25)
    gb = (2 * (gb >= 0) - 1) * jnp.maximum(jnp.abs(gb), 0.25)
    h = _layernorm(x, axis=-1) * (1 + ca) + sa
    x = x + ga * _L0_attn_ref(h, L0_attn_qkv_w, L0_attn_qkv_b, L0_attn_proj_w, L0_attn_proj_b)
    h = _layernorm(x, axis=-1) * (1 + cb) + sb
    x = x + gb * _L0_ffn_ref(h, L0_ffn_router_w, L0_ffn_expert_bias, L0_ffn_w_gate, L0_ffn_w_down, L0_ffn_w_gate_shared, L0_ffn_w_down_shared)
    return x

_drawn_inputs = setup_inputs


def setup_inputs(seed=0):
    import zlib

    import numpy as np

    out = dict(_drawn_inputs(seed))
    spreads = {'L0_ffn_expert_bias': (0.0, 0.8)}
    factors = {'L0_attn_qkv_w': 5.559,
     'L0_attn_qkv_b': 6.662,
     'L0_attn_proj_w': 4.401,
     'L0_attn_proj_b': 4.331,
     'L0_ffn_router_w': 8.0,
     'L0_ffn_w_gate': 8.0,
     'L0_ffn_w_down': 8.0,
     'L0_ffn_w_gate_shared': 8.0,
     'L0_ffn_w_down_shared': 8.0,
     'L0_c': 3.022,
     'L0_wmod': 2.897}
    for name, (base, spread) in spreads.items():
        noise = np.random.default_rng([zlib.crc32(name.encode()), seed]).standard_normal(out[name].shape)
        drawn = base * np.exp(spread * noise) if base else spread * noise
        out[name] = jnp.asarray(drawn.astype(out[name].dtype))
    for name, factor in factors.items():
        out[name] = (out[name] * factor).astype(out[name].dtype)
    return out
```

```python
from contextlib import ExitStack

import concourse.bass as bass
import concourse.mybir as mybir
from concourse.alu_op_type import AluOpType as ALU

F32, BF16, I32, U32 = mybir.dt.float32, mybir.dt.bfloat16, mybir.dt.int32, mybir.dt.uint32
ACT = mybir.ActivationFunctionType
AX = mybir.AxisListType

P = 128
NB, S, D = 16, 512, 128
NT = S // P
H, HD = 16, 8
NE, TOPK, INTER = 160, 8, 64
NPAGE = NE + NB * S * TOPK // P
GRP = 4
NGRP = NPAGE // GRP
PCOL = -(-NPAGE // P)
SLOTS = 8
MAXROW = 48
Q_RUNS = ((0, (0, 0, 0)), (3, (1, 1)), (5, (2,)))
K_RUNS = ((0, (0, 1, 2)), (3, (0, 1)), (5, (0,)))
EPS = 1e-5
SCALE = 1.0 / HD ** 0.5
NEG = -3.0e38
WROW = INTER + D


class Events:

    def __init__(self, sem, names):
        self.sem, self.names, self.k = sem, names, 0

    def done(self, ins, name):
        assert self.names[self.k % len(self.names)] == name, (name, self.names[self.k % len(self.names)])
        self.k += 1
        ins.then_inc(self.sem, 1)

    def wait(self, eng, name, n):
        wait(eng, self.sem, n * len(self.names) + self.names.index(name) + 1)


def wait(eng, sem, value):
    if not isinstance(value, int) or value > 0:
        eng.wait_ge(sem, value)
    if not isinstance(value, int) and eng.engine == mybir.EngineType.SP:
        apart(eng)


def apart(eng):
    eng.nop(nofuse=True)


def merge(*streams):
    timed = []
    for order, (steps, start, end, *lag) in enumerate(streams):
        share = (end - start) / len(steps)
        for k, step in enumerate(steps):
            for j, (name, f) in enumerate(step.items()):
                at = start + share * (k + 0.5 + j * (lag[0] if lag else 0.9) / max(len(step) - 1, 1))
                timed.append((at, order, k, j, {name: f}))
    return [t[-1] for t in sorted(timed, key=lambda t: t[:4])]


def run(eng_name, eng, steps):
    for step in steps:
        if eng_name in step:
            step[eng_name](eng)


def build(nc, x, wts, bvec, brow, wexp, wds, const, constb, out):
    with ExitStack() as ctx:
        def sb(name, shape, dt=F32):
            return ctx.enter_context(nc.sbuf_tensor(name, shape, dt))

        def sem(name):
            return ctx.enter_context(nc.semaphore(name))

        qd = nc.dram_tensor("q_stacks", (NB, 2, 64, 8 * S), BF16, kind="Internal").ap()
        kd = nc.dram_tensor("k_stacks", (NB, 2, 64, 8 * S), BF16, kind="Internal").ap()
        pages = nc.dram_tensor("pages", (NPAGE * P, D), F32, kind="Internal").ap()
        ends_d = nc.dram_tensor("page_ends", (1, NB * NE), F32, kind="Internal").ap()
        table_d = nc.dram_tensor("page_table", (PCOL * P,), I32, kind="Internal").ap()

        nw = wts.shape[1]
        w_all = sb("w_all", [P, nw])
        col = {}
        at = 0
        for name, width in (("wq", D), ("wqr", D), ("wk", D), ("wkr", D), ("wv", D), ("wp", D), ("rw", NE),
                            ("wmod", 6 * D), ("cT", NB), ("wgs", INTER), ("bq", 1), ("bqr", 1), ("bk", 1),
                            ("bkr", 1), ("bp", 1)):
            col[name] = w_all[:, at:at + width]
            at += width
        assert at == nw
        bv_bc = sb("bv_bc", [P, D])
        eb_row = sb("eb_row", [1, NE])
        wds_sb = sb("wds_sb", [INTER, D])
        c_all = sb("c_all", [P, const.shape[1]])
        cosT, sinT = c_all[:, 0:S], c_all[:, S:2 * S]
        ident = c_all[:, 2 * S:2 * S + P]
        iota_e = c_all[:, 2 * S + P:2 * S + P + NE]
        page_no = c_all[:, 2 * S + P + NE:2 * S + P + NE + PCOL]
        cb_all = sb("cb_all", [P, 5 * P], BF16)
        mask_q, mask_k, identb, upper, onesb = (cb_all[:, i * P:(i + 1) * P] for i in range(5))
        ones_row = sb("ones_row", [1, P])
        zero_row = sb("zero_row", [1, NE])
        zerob = sb("zerob", [P, S], BF16)
        oneb = sb("oneb", [P, S], BF16)
        mhalf = sb("mhalf", [P, NT])
        silu_c = sb("silu_c", [P, NB])
        sig_c = sb("sig_c", [P, NB])
        mod = sb("mod", [P, 6, NB])
        gsign = sb("gsign", [P, 2, NB])
        gabs = sb("gabs", [P, 2, NB])
        gneg = sb("gneg", [P, 2, NB])
        ga_bp = sb("ga_bp", [P, NB])

        xr = sb("xr", [P, NB * NT, D])
        vh = sb("vh", [P, NB, S])
        pos_all = sb("pos_all", [P, NB * NT, TOPK], U32)
        v8_all = sb("v8_all", [P, NB * NT * TOPK])

        qm = sb("qm", [P, 2, 2, S], BF16)
        km = sb("km", [P, 2, 2, S], BF16)
        qe = sb("qe", [P, 2, 2, S], BF16)
        ke = sb("ke", [P, 2, 2, S], BF16)
        prob = sb("prob", [P, 20, S])
        v_ext = sb("v_ext", [P, NT, H, 32])
        stat = sb("stat", [P, NT, 6])
        mv = sb("mv", [P, NT, 2])
        var = sb("var", [P, NT])
        rstd = sb("rstd", [P, NT])
        xn = sb("xn", [P, NT, D])
        hT = sb("hT", [P, S])
        rot_a = sb("rot_a", [P, S])
        rot_b = sb("rot_b", [P, S])
        full = sb("full", [P, S])
        rest = sb("rest", [P, S])
        part = {"q": sb("q_part", [P, 3, S], BF16), "k": sb("k_part", [P, 3, S], BF16)}
        rmax = sb("rmax", [P, 2, 8, NT])
        rmax_rest = sb("rmax_rest", [P, 64])
        rmax_part = sb("rmax_part", [P, 3, 64], BF16)
        rmax_T = sb("rmax_T", [64, 3 * P], BF16)
        oT = sb("oT", [P, 2, S])
        rden = sb("rden", [P, NT, 4])
        onorm = sb("onorm", [P, NT, D])
        on_att = sb("on_att", [P, 2, S])
        onT, att = on_att[:, 0, :], on_att[:, 1, :]
        stat2 = sb("stat2", [P, NT, 6])
        mv2 = sb("mv2", [P, NT, 2])
        var2 = sb("var2", [P, NT])
        rstd2 = sb("rstd2", [P, NT])
        xn2 = sb("xn2", [P, NT, D])
        h2T = sb("h2T", [P, S])
        h2 = sb("h2", [P, NT, D])
        logit = sb("logit", [P, NT, NE])
        logit_cut = on_att[:, :, :].rearrange("p a t -> p (a t)")[:, 0:NT * NE].rearrange("p (t k) -> p t k", k=NE)
        chosen = sb("chosen", [P, NT, NE], BF16)
        v8 = sb("v8", [P, NT, TOPK])
        i8 = sb("i8", [P, NT, TOPK], U32)
        i8f = sb("i8f", [P, NT, TOPK])
        pos8 = sb("pos8", [P, NT, TOPK])
        pos_s = sb("pos_s", [P, NT * TOPK], U32)
        step_p = sb("step_p", [P, 2, NE])
        place = xn2[:, :, :].rearrange("p t d -> p (t d)")[:, 0:2 * NE].rearrange("p (t k) -> p t k", k=NE)
        junk = on_att[:, :, :].rearrange("p a t -> p (a t)").bitcast(BF16)[:, 0:TOPK * NE] \
            .rearrange("p (k e) -> p k e", k=TOPK)
        page_bc = sb("page_bc", [P, 2, NE])
        rows = sb("rows", [1, 3, NE])
        fill = sb("fill", [1, NE])
        total = sb("total", [1, NE])
        total_i = sb("total_i", [1, NE], I32)
        full_i = sb("full_i", [1, NE], I32)
        newp = sb("newp", [1, NE])
        endp = sb("endp", [1, NE])
        cur = sb("cur", [1, NE])
        curd = sb("curd", [1, NE])
        nextp = sb("nextp", [1, 1])

        bank = [ctx.enter_context(nc.psum_tensor(f"bank{i}", [P, 512], F32)) for i in range(8)]
        MX, ST, PV, MA, MB = bank[0:2], bank[2:5], bank[5], bank[6], bank[7]

        s_const, s_x, s_zero, s_set, s_zfill, s_rest = (
            sem(n) for n in ("s_const", "s_x", "s_zero", "s_set", "s_zfill", "s_rest"))
        s_modd, s_modp, s_moda = sem("s_modd"), sem("s_modp"), sem("s_moda")
        pre_d = Events(sem("pre_d"), ["stats", "aggr", "var", "xn", "q_a", "q_b", "q", "k_a", "k_b", "k", "v"])
        pre_g = Events(sem("pre_g"), ["rstd", "q_rest", "q_3", "k_rest", "k_3"])
        pre_a = Events(sem("pre_a"), ["hT", "q_1", "q_2", "k_1", "k_2"])
        pre_p = Events(sem("pre_p"), ["T", "q_a", "q_b", "k_a", "k_b", "v"])
        s_store = {"q": sem("s_store_q"), "k": sem("s_store_k")}
        s_mxp, s_mxd = sem("s_mxp"), sem("s_mxd")
        fin_d = Events(sem("fin_d"), ["m1", "rest", "m2", "m3"])
        s_finp, s_fina, s_mstore = sem("s_finp"), sem("s_fina"), sem("s_mstore")
        s_ldm = [sem(f"s_ldm{c}") for c in range(4)]
        s_lde = [sem(f"s_lde{c}") for c in range(4)]
        s_exp, s_exa = sem("s_exp"), sem("s_exa")
        s_pv, s_ov, s_ot, s_rd, s_on, s_vx = (sem(n) for n in ("s_pv", "s_ov", "s_ot", "s_rd", "s_on", "s_vx"))
        post_p = Events(sem("post_p"), ["onT", "proj", "attT", "h2T", "log0", "log1", "cnt", "bc", "z0", "z1", "h2"])
        post_a = Events(sem("post_a"), ["onT", "att", "h2T", "h2T_keep", "log0", "log1", "bc", "h2"])
        post_d = Events(sem("post_d"), ["x1", "stats", "aggr", "var", "xn", "v8", "i8", "cut", "chosen",
                                        "i8f", "v8_keep", "total", "total_i", "full_i", "newp", "endp",
                                        "curd0", "jump0", "jump", "openrow", "filled", "fill", "curd1", "curd2", "cur", "nextp",
                                        "step0", "zs0", "place0", "pick0", "pos0", "step1", "zs1", "place1", "pick1", "pos1",
                                        "pos_s", "pos_keep"])
        post_g = Events(sem("post_g"), ["rstd"])
        s_scat = sem("s_scat")
        s_ends = sem("s_ends")
        s_tab, s_tabd, s_tabp = sem("s_tab"), sem("s_tabd"), sem("s_tabp")
        s_out = sem("s_out")

        ZROWS = 56
        NZ = NPAGE // ZROWS
        setup = [
            {"sp": lambda e: [
                e.dma_start(xr[:, 0:NT, :], x[0].rearrange("(t p) d -> p t d", p=P)).then_inc(s_x, 16),
                e.dma_start(w_all[:, :], wts).then_inc(s_const, 16),
                e.dma_start(c_all[:, :], const).then_inc(s_const, 16),
                e.dma_start(cb_all[:, :], constb).then_inc(s_const, 16),
                e.dma_start(bv_bc[:, :], bvec.partition_broadcast(P)).then_inc(s_const, 16),
                e.dma_start(eb_row[:, :], brow).then_inc(s_const, 16),
                e.dma_start(wds_sb[:, :], wds).then_inc(s_const, 16),
                e.wait_ge(s_set, 2),
                [e.dma_start(d[:, :, MAXROW:64].rearrange("n a r (g t) -> (r g) (n a) t", t=S),
                             src[:, :].rearrange("p (o t) -> p o t", o=1).broadcast_to([P, 2 * NB, S]))
                 .then_inc(s_rest, 16) for d, src in ((qd, zerob), (kd, oneb))],
                e.wait_ge(s_x, 16),
                e.dma_start(xr[:, NT:, :].rearrange("p (n t) d -> p n t d", t=NT),
                            x[1:NB].rearrange("n (t p) d -> p n t d", p=P)).then_inc(s_x, 16)]},
            {"pool": lambda e: [
                e.memset(prob[:, :, :], 0.0).then_inc(s_zero, 1),
                e.memset(v_ext[:, :, :, :], 0.0).then_inc(s_zero, 1),
                e.wait_ge(s_zero, 2),
                e.memset(v_ext[:, :, :, HD:HD + 1], 1.0).then_inc(s_zero, 1)],
             "dve": lambda e: [
                e.memset(zerob[:, :], 0.0).then_inc(s_set, 1),
                e.memset(oneb[:, :], 1.0).then_inc(s_set, 1),
                e.memset(mhalf[:, :], -0.5).then_inc(s_set, 1),
                e.memset(ones_row[:, :], 1.0).then_inc(s_set, 1),
                e.memset(zero_row[:, :], 0.0).then_inc(s_set, 1),
                e.memset(fill[:, :], 0.0).then_inc(s_set, 1),
                e.memset(nextp[:, :], float(NE)).then_inc(s_set, 1),
                e.wait_ge(s_const, 96),
                e.tensor_copy(cur[:, :], iota_e[0:1, :]).then_inc(s_set, 1)]},
            {"act": lambda e: [
                e.wait_ge(s_zero, 1),
                [e.dma_start(pages[z * ZROWS * P:(z + 1) * ZROWS * P, :].rearrange("(p r) d -> p (r d)", p=P),
                             prob[:, :, :].rearrange("p a b -> p (a b)")[:, 0:ZROWS * D]).then_inc(s_zfill, 16)
                 for z in range(NZ)]]},
            {"act": lambda e: [e.wait_ge(s_const, 96),
                               e.activation(sig_c[:, :], col["cT"], ACT.Exp, scale=-1.0).then_inc(s_moda, 1)]},
            {"dve": lambda e: [e.wait_ge(s_moda, 1),
                               e.tensor_scalar(sig_c[:, :], sig_c[:, :], 1.0, None, ALU.add).then_inc(s_modd, 1),
                               e.wait_ge(s_modd, 1),
                               e.reciprocal(sig_c[:, :], sig_c[:, :]).then_inc(s_modd, 1),
                               e.wait_ge(s_modd, 2),
                               e.tensor_tensor(silu_c[:, :], sig_c[:, :], col["cT"], ALU.mult).then_inc(s_modd, 1)]},
            {"pe": lambda e: [e.wait_ge(s_modd, 3),
                              [e.matmul(MA[:, j * NB:(j + 1) * NB], col["wmod"][:, j * D:(j + 1) * D], silu_c[:, :],
                                        start=True, stop=True) for j in range(6)][-1].then_inc(s_modp, 1)]},
            {"dve": lambda e: [
                e.wait_ge(s_modp, 1),
                e.tensor_copy(mod[:, :, :], MA[:, 0:6 * NB].rearrange("p (j n) -> p j n", n=NB)).then_inc(s_modd, 1),
                e.wait_ge(s_modd, 4),
                e.tensor_scalar(gsign[:, :, :], mod[:, 2::3, :], 0.0, 2.0, ALU.is_ge, ALU.mult).then_inc(s_modd, 1),
                e.tensor_scalar(gneg[:, :, :], mod[:, 2::3, :], -1.0, 0.25, ALU.mult, ALU.max).then_inc(s_modd, 1),
                e.wait_ge(s_modd, 6),
                e.tensor_tensor(gabs[:, :, :], mod[:, 2::3, :], gneg[:, :, :], ALU.max).then_inc(s_modd, 1),
                e.wait_ge(s_modd, 7),
                e.scalar_tensor_tensor(out=mod[:, 2::3, :], in0=gsign[:, :, :], scalar=-1.0, in1=gabs[:, :, :],
                                       op0=ALU.add, op1=ALU.mult).then_inc(s_modd, 1),
                e.tensor_scalar(mod[:, 1::3, :], mod[:, 1::3, :], 1.0, None, ALU.add).then_inc(s_modd, 1),
                e.wait_ge(s_modd, 9),
                e.tensor_scalar(ga_bp[:, :], mod[:, 2, :], col["bp"], None, ALU.mult).then_inc(s_modd, 1)]},
        ]
        MODDONE = 10

        def xtile(n, t):
            return xr[:, bass.ds(n * NT + t, 1), :].rearrange("p o d -> p (o d)")

        def seq(n):
            return xr[:, bass.ds(n * NT, NT), :]

        def mcol(j, n):
            return mod[:, j, bass.ds(n, 1)]

        def pre(n):
            steps = []

            def ln(e):
                if isinstance(n, int):
                    e.wait_ge(s_x, 16 if n == 0 else 32)
                pre_d.wait(e, "v", n - 1)
                apart(e)
                for t in range(NT):
                    last = e.bn_stats(stat[:, t, :], xtile(n, t))
                pre_d.done(last, "stats")
                pre_d.wait(e, "stats", n)
                apart(e)
                for t in range(NT):
                    last = e.bn_aggr(mv[:, t, :], stat[:, t, :])
                pre_d.done(last, "aggr")
                pre_d.wait(e, "aggr", n)
                pre_d.done(e.tensor_scalar(var[:, :], mv[:, :, 1], EPS, None, ALU.add), "var")

            def rs(e):
                pre_d.wait(e, "var", n)
                if isinstance(n, int) and n == 0:
                    e.wait_ge(s_set, 3)
                pre_g.done(e.tensor_tensor(rstd[:, :], var[:, :], mhalf[:, :], ALU.pow), "rstd")
            steps.append({"dve": ln, "pool": rs})

            def norm(e):
                pre_g.wait(e, "rstd", n)
                pre_p.wait(e, "T", n - 1)
                for t in range(NT):
                    last = e.tensor_scalar(xn[:, t, :], xtile(n, t), mv[:, t, 0:1], rstd[:, t:t + 1],
                                           ALU.subtract, ALU.mult)
                pre_d.done(last, "xn")

            def tr(e):
                pre_d.wait(e, "xn", n)
                if isinstance(n, int) and n == 0:
                    e.wait_ge(s_const, 96)
                    e.wait_ge(s_modd, MODDONE)
                for t in range(NT):
                    last = e.transpose(MA[:, t * P:(t + 1) * P], xn[:, t, :], ident)
                pre_p.done(last, "T")

            def modulate(e):
                pre_p.wait(e, "T", n)
                pre_a.done(e.activation(hT[:, :], MA[:, :], ACT.Identity, bias=mcol(0, n), scale=mcol(1, n)), "hT")
            steps.append({"dve": norm, "pe": tr, "act": modulate})

            stores = []
            for w, prev in (("q", None), ("k", "q")):
                def proj_a(e, w=w, prev=prev):
                    if prev is None:
                        pre_a.wait(e, "hT", n)
                    else:
                        pre_d.wait(e, prev + "_b", n)
                    pre_p.done(e.matmul(MA[:, :], col["w" + w], hT[:, :], start=True, stop=True), w + "_a")

                def rope_a(e, w=w):
                    pre_p.wait(e, w + "_a", n)
                    if w == "k":
                        pre_d.wait(e, "q", n)
                    pre_d.done(e.scalar_tensor_tensor(out=rot_a[:, :], in0=MA[:, :], scalar=col["b" + w], in1=cosT,
                                                      op0=ALU.add, op1=ALU.mult), w + "_a")

                def proj_b(e, w=w):
                    pre_d.wait(e, w + "_a", n)
                    pre_p.done(e.matmul(MA[:, :], col["w" + w + "r"], hT[:, :], start=True, stop=True), w + "_b")

                def rope_b(e, w=w):
                    pre_p.wait(e, w + "_b", n)
                    pre_d.done(e.scalar_tensor_tensor(out=rot_b[:, :], in0=MA[:, :], scalar=col["b" + w + "r"],
                                                      in1=sinT, op0=ALU.add, op1=ALU.mult), w + "_b")
                    pre_d.wait(e, w + "_b", n)
                    pre_g.wait(e, "k_rest" if w == "q" else "q_rest", n - 1 if w == "q" else n)
                    pre_d.done(e.tensor_tensor(full[:, :], rot_a[:, :], rot_b[:, :], ALU.add), w)

                def part1(e, w=w):
                    pre_d.wait(e, w, n)
                    wait(e, s_store[w], 16 * 6 * n)
                    pre_a.done(e.activation(part[w][:, 0, :], full[:, :], ACT.Identity), w + "_1")

                def rest1(e, w=w):
                    pre_a.wait(e, w + "_1", n)
                    pre_g.wait(e, "k_3" if w == "q" else "q_3", n - 1 if w == "q" else n)
                    pre_g.done(e.tensor_tensor(rest[:, :], full[:, :], part[w][:, 0, :], ALU.subtract),
                               w + "_rest")

                def part2(e, w=w):
                    pre_g.wait(e, w + "_rest", n)
                    pre_a.done(e.activation(part[w][:, 1, :], rest[:, :], ACT.Identity), w + "_2")

                def part3(e, w=w):
                    pre_a.wait(e, w + "_2", n)
                    pre_g.done(e.tensor_tensor(part[w][:, 2, :], rest[:, :], part[w][:, 1, :], ALU.subtract),
                               w + "_3")

                def store(e, w=w):
                    pre_g.wait(e, w + "_3", n)
                    stacks = (qd if w == "q" else kd)[bass.ds(n, 1)].rearrange("o a r (g t) -> (o a) r g t", t=S)
                    for first, parts in (Q_RUNS if w == "q" else K_RUNS):
                        m = len(parts)
                        for par in range(2):
                            dst = stacks[par, first * 8:(first + m) * 8].rearrange("(s r) g t -> (r g) s t", s=m)
                            src = part[w][par * 64:(par + 1) * 64, parts[0]:parts[0] + (1 if w == "q" else m), :]
                            e.dma_start(dst, src.broadcast_to([64, m, S]) if w == "q" and m > 1 else src) \
                             .then_inc(s_store[w], 16)
                steps.append({"pe": proj_a, "dve": rope_a})
                steps.append({"pe": proj_b, "dve": rope_b})
                steps.append({"act": part1, "pool": rest1})
                steps.append({"act": part2, "pool": part3})
                stores.append({"sp": store})

            def v_proj(e):
                pre_d.wait(e, "k_b", n)
                for t in range(NT):
                    last = e.matmul(MA[:, t * P:(t + 1) * P], hT[:, t * P:(t + 1) * P], col["wv"],
                                    start=True, stop=True)
                pre_p.done(last, "v")

            def v_keep(e):
                pre_p.wait(e, "v", n)
                pre_d.done(e.tensor_tensor(
                    vh[:, bass.ds(n, 1), :].rearrange("p o (t d) -> p (o t) d", d=D),
                    MA[:, :].rearrange("p (t d) -> p t d", d=D),
                    bv_bc[:, :].rearrange("p (o d) -> p o d", o=1).broadcast_to([P, NT, D]), ALU.add), "v")
            steps.insert(len(steps) - 2, {"pe": v_proj, "dve": v_keep})
            steps = steps[:7] + stores[0:1] + steps[7:] + stores[1:2]
            return steps

        def max_units(c):
            heads = [(h, par) for par in range(2) for h in range(2)]
            units = [(3, [hp]) for hp in heads] + [(2, [hp]) for hp in heads]
            units += [(1, [(0, par), (1, par)]) for par in range(2)]
            return units + [(0, [(0, par), (1, par)]) for par in range(2)]

        NU = 12

        def max_loads(n, quads):
            def load(e, c):
                if isinstance(n, int) and n == 0 and c == 0:
                    e.wait_ge(s_rest, 32)
                for w in "qk":
                    wait(e, s_store[w], 16 * 6 * (n + 1))
                wait(e, s_mxp, n * 4 * NU + (c - 1) * NU)
                e.dma_start(qm[:, c % 2, :, :].rearrange("p h t -> p (h t)"), stack(qd, n, c)).then_inc(s_ldm[c], 16)
                e.dma_start(km[:, c % 2, :, :].rearrange("p h t -> p (h t)"), stack(kd, n, c)).then_inc(s_ldm[c], 16)
            return [{"sp": lambda e, c=c: load(e, c)} for c in quads]

        def mx(n):
            steps = []
            for c in range(4):
                for u, (i, heads) in enumerate(max_units(c)):
                    g = c * NU + u
                    width = (i + 1) * P

                    def scores(e, c=c, u=u, i=i, heads=heads, g=g, width=width):
                        if u == 0:
                            e.wait_ge(s_ldm[c], 32 * (n + 1))
                        if g < 2:
                            wait(e, s_fina, n)
                        else:
                            wait(e, s_mxd, n * 4 * NU + g - 1)
                        for k, (h, par) in enumerate(heads):
                            rows_ = slice(64 * par, 64 * par + 64)
                            e.matmul(MX[g % 2][:, k * width:(k + 1) * width],
                                     qm[rows_, c % 2, h, i * P:(i + 1) * P], km[rows_, c % 2, h, 0:width],
                                     start=True, stop=True)
                            last = e.matmul(MX[g % 2][:, (k + 1) * width - P:(k + 1) * width], identb, mask_q,
                                            start=False, stop=True, skip_group_check=True)
                        last.then_inc(s_mxp, 1)

                    def reduce(e, c=c, i=i, heads=heads, g=g, width=width):
                        e.wait_ge(s_mxp, n * 4 * NU + g + 1)
                        if g == 0:
                            fin_d.wait(e, "rest", n - 1)
                        h, par = heads[0]
                        e.tensor_reduce(rmax[:, par, 2 * c + h:2 * c + h + len(heads), i],
                                        MX[g % 2][:, 0:len(heads) * width].rearrange("p (k w) -> p k w", w=width),
                                        AX.X, ALU.max).then_inc(s_mxd, 1)
                    steps.append({"pe": scores, "dve": reduce})
                    if u == 1 and c in (1, 2):
                        steps += max_loads(n, [c + 1])

            def split(e):
                flat = rmax[:, :, :, :].rearrange("p a h i -> p (a h i)")
                e.wait_ge(s_mxd, (n + 1) * 4 * NU)
                wait(e, s_finp, n)
                fin_d.done(e.tensor_scalar(rmax_part[:, 0, :], flat, -1.0, None, ALU.mult), "m1")
                fin_d.wait(e, "m1", n)
                fin_d.done(e.scalar_tensor_tensor(out=rmax_rest[:, :], in0=flat, scalar=-1.0,
                                                  in1=rmax_part[:, 0, :], op0=ALU.mult, op1=ALU.subtract), "rest")
                fin_d.wait(e, "rest", n)
                fin_d.done(e.tensor_copy(rmax_part[:, 1, :], rmax_rest[:, :]), "m2")
                fin_d.wait(e, "m2", n)
                fin_d.done(e.tensor_tensor(rmax_part[:, 2, :], rmax_rest[:, :], rmax_part[:, 1, :],
                                           ALU.subtract), "m3")

            mx_b = MX[0][:, :].bitcast(BF16)

            def turn(e):
                fin_d.wait(e, "m3", n)
                apart(e)
                for j in range(3):
                    last = e.transpose(mx_b[0:64, j * P:(j + 1) * P], rmax_part[:, j, :], identb)
                last.then_inc(s_finp, 1)

            def keep(e):
                e.wait_ge(s_finp, n + 1)
                wait(e, s_mstore, 32 * n)
                e.activation(rmax_T[:, :], mx_b[0:64, 0:3 * P], ACT.Identity).then_inc(s_fina, 1)

            def store(e):
                wait(e, s_fina, n + 1)
                for par in range(2):
                    dst = qd[bass.ds(n, 1), par].rearrange("o r t -> (o r) t")[MAXROW:MAXROW + 3, :]
                    e.dma_start(dst.rearrange("r (g t) -> g r t", t=P),
                                rmax_T[32 * par:32 * par + 32, :].rearrange("g (r t) -> g r t", t=P)) \
                     .then_inc(s_mstore, 16)
            steps.append({"dve": split, "pe": turn, "act": keep, "sp": store})
            return steps

        def stack(d, n, c):
            return d[bass.ds(n, 1)].rearrange("o a r t -> (o a r) t")[:, 2 * c * S:(2 * c + 2) * S]

        EU = 10
        def exp_place(h, par, j):
            if j == 0:
                return 4 * par + 2 * h, 0
            if j == 1:
                return 4 * par + 2 * h + 1, 0
            if j == 3:
                return 4 * par + 2 * h + 1, 3 * P
            return 8 + par, 2 * P * h

        def exp_loads(n, quads):
            def load(e, c):
                wait(e, s_mstore, 32 * (n + 1))
                wait(e, s_exp, n * 4 * EU + (c - 1) * EU)
                e.dma_start(qe[:, c % 2, :, :].rearrange("p h t -> p (h t)"), stack(qd, n, c)).then_inc(s_lde[c], 16)
                e.dma_start(ke[:, c % 2, :, :].rearrange("p h t -> p (h t)"), stack(kd, n, c)).then_inc(s_lde[c], 16)
            return [{"sp": lambda e, c=c: load(e, c)} for c in quads]

        def ex(n):
            steps = []

            def prev_user(g):
                if g >= 3:
                    return 3
                return g + 4 * EU - max(k for k in range(4 * EU) if k % 3 == g % 3)

            def pv(c):
                def vx(e):
                    wait(e, s_pv, 4 * (n - 1) + c + 1)
                    if isinstance(n, int) and n == 0:
                        e.wait_ge(s_zero, 3)
                    pre_d.wait(e, "v", n)
                    e.tensor_copy(v_ext[:, :, 4 * c:4 * c + 4, 0:HD],
                                  vh[:, bass.ds(n, 1), :].rearrange("p o (t h d) -> p (o t) h d", t=NT, d=HD)
                                  [:, :, 4 * c:4 * c + 4, :]).then_inc(s_vx, 1)

                def product(e):
                    e.wait_ge(s_exa, n * 4 * EU + (c + 1) * EU)
                    e.wait_ge(s_vx, 4 * n + c + 1)
                    wait(e, s_on, 4 * n + c)
                    for j in range(NT):
                        for g in range(4):
                            u, c0 = exp_place(g // 2, g % 2, j)
                            last = e.matmul(PV[32 * g:32 * g + 32, j * P:S], v_ext[:, j, 4 * c + g, :],
                                            prob[:, (c % 2) * EU + u, c0:c0 + S - j * P],
                                            start=(j == 0), stop=(j == NT - 1), skip_group_check=True)
                    last.then_inc(s_pv, 1)

                def take(e):
                    e.wait_ge(s_pv, 4 * n + c + 1)
                    wait(e, s_ot, 4 * n + c - 1)
                    e.activation(oT[:, c % 2, :], PV[:, :], ACT.Identity).then_inc(s_ov, 1)

                def turn(e):
                    e.wait_ge(s_ov, 4 * n + c + 1)
                    for t in range(NT):
                        last = e.transpose(PV[:, t * P:(t + 1) * P], oT[:, c % 2, t * P:(t + 1) * P], ident)
                    last.then_inc(s_ot, 1)

                def norm(e):
                    heads = PV[:, :].rearrange("p (t g d) -> p t g d", t=NT, g=4)
                    e.wait_ge(s_ot, 4 * n + c + 1)
                    wait(e, s_on, 4 * n + c)
                    e.reciprocal(rden[:, :, :], heads[:, :, :, HD]).then_inc(s_rd, 1)
                    e.wait_ge(s_rd, 4 * n + c + 1)
                    if c == 0:
                        post_p.wait(e, "onT", n - 1)
                    e.tensor_tensor(onorm[:, :, 32 * c:32 * c + 32].rearrange("p t (g d) -> p t g d", g=4),
                                    heads[:, :, :, 0:HD],
                                    rden[:, :, :].rearrange("p t (g o) -> p t g o", o=1)
                                    .broadcast_to([P, NT, 4, HD]), ALU.mult).then_inc(s_on, 1)
                return [{"pool": vx}, {"pe": product, "act": take}, {"pe": turn, "dve": norm}]

            todo = []
            for c in range(4):
                units = {}
                for par in range(2):
                    for h in range(2):
                        for j in range(NT):
                            u, c0 = exp_place(h, par, j)
                            units.setdefault(u, []).append((h, par, j, c0))
                for u in range(EU):
                    g = c * EU + u

                    def scores(e, c=c, u=u, g=g, pieces=units[u]):
                        if u == 0:
                            e.wait_ge(s_lde[c], 32 * (n + 1))
                        wait(e, s_exa, n * 4 * EU + g - prev_user(g) + 1)
                        for (h, par, j, c0) in pieces:
                            rows_ = slice(64 * par, 64 * par + 64)
                            e.matmul(ST[g % 3][:, c0:c0 + S - j * P], ke[rows_, c % 2, h, j * P:(j + 1) * P],
                                     qe[rows_, c % 2, h, j * P:S], start=True, stop=True)
                            last = e.matmul(ST[g % 3][:, c0:c0 + P], identb, mask_k, start=False, stop=True,
                                            skip_group_check=True)
                        last.then_inc(s_exp, 1)

                    def expo(e, c=c, u=u, g=g):
                        e.wait_ge(s_exp, n * 4 * EU + g + 1)
                        if u == 0:
                            wait(e, s_pv, 4 * n + c - 1)
                            if isinstance(n, int) and n == 0 and c == 0:
                                e.wait_ge(s_zfill, 16 * NZ)
                        e.activation(prob[:, (c % 2) * EU + u, :], ST[g % 3][:, :], ACT.Exp, scale=SCALE) \
                         .then_inc(s_exa, 1)
                    steps.append({"pe": scores, "act": expo})
                    if c > 0 and u in (2, 4, 6):
                        steps.append(todo.pop(0))
                todo += pv(c)
            return steps + todo

        def scatter(e, n, t, k):
            if t == 0 and k == 0:
                post_d.wait(e, "pos_s", n)
                post_a.wait(e, "h2", n)
                if isinstance(n, int) and n == 0:
                    e.wait_ge(s_zfill, 16 * NZ)
                apart(e)
            e.indirect_dma_start(
                out=pages, in_=h2[:, t, :], in_offset=None,
                out_offset=bass.IndirectOffsetOnAxis(ap=pos_s[:, t * TOPK + k:t * TOPK + k + 1], axis=0),
            ).then_inc(s_scat, 16)

        def post(n):
            steps = []
            P_, A_, D_, G_ = post_p, post_a, post_d, post_g

            def on_turn(e):
                e.wait_ge(s_on, 4 * (n + 1))
                A_.wait(e, "h2", n - 1)
                for t in range(NT):
                    last = e.transpose(MB[:, t * P:(t + 1) * P], onorm[:, t, :], ident)
                P_.done(last, "onT")

            def on_keep(e):
                P_.wait(e, "onT", n)
                D_.wait(e, "pos1", n - 1)
                A_.done(e.activation(onT, MB[:, :], ACT.Identity), "onT")
            steps.append({"pe": on_turn, "act": on_keep})

            def proj(e):
                A_.wait(e, "onT", n)
                P_.done(e.matmul(MB[:, :], col["wp"], onT, start=True, stop=True), "proj")

            def gate(e):
                P_.wait(e, "proj", n)
                A_.done(e.activation(att, MB[:, :], ACT.Identity, bias=ga_bp[:, bass.ds(n, 1)],
                                     scale=mcol(2, n)), "att")
            steps.append({"pe": proj, "act": gate})

            def att_turn(e):
                A_.wait(e, "att", n)
                for t in range(NT):
                    last = e.transpose(MB[:, t * P:(t + 1) * P], att[:, t * P:(t + 1) * P], ident)
                P_.done(last, "attT")

            def residual(e):
                P_.wait(e, "attT", n)
                D_.done(e.tensor_tensor(seq(n), seq(n), MB[:, :].rearrange("p (t d) -> p t d", d=D), ALU.add), "x1")
                D_.wait(e, "x1", n)
                apart(e)
                for t in range(NT):
                    last = e.bn_stats(stat2[:, t, :], xtile(n, t))
                D_.done(last, "stats")
                D_.wait(e, "stats", n)
                apart(e)
                for t in range(NT):
                    last = e.bn_aggr(mv2[:, t, :], stat2[:, t, :])
                D_.done(last, "aggr")
                D_.wait(e, "aggr", n)
                D_.done(e.tensor_scalar(var2[:, :], mv2[:, :, 1], EPS, None, ALU.add), "var")

            def rs(e):
                D_.wait(e, "var", n)
                G_.done(e.tensor_tensor(rstd2[:, :], var2[:, :], mhalf[:, :], ALU.pow), "rstd")
            steps.append({"pe": att_turn, "dve": residual, "pool": rs})

            def norm(e):
                G_.wait(e, "rstd", n)
                for t in range(NT):
                    last = e.tensor_scalar(xn2[:, t, :], xtile(n, t), mv2[:, t, 0:1], rstd2[:, t:t + 1],
                                           ALU.subtract, ALU.mult)
                D_.done(last, "xn")

            def turn(e):
                D_.wait(e, "xn", n)
                for t in range(NT):
                    last = e.transpose(MB[:, t * P:(t + 1) * P], xn2[:, t, :], ident)
                P_.done(last, "h2T")

            def modulate(e):
                P_.wait(e, "h2T", n)
                A_.done(e.activation(h2T[:, :], MB[:, :], ACT.Identity, bias=mcol(3, n), scale=mcol(4, n)), "h2T")
                wait(e, s_vx, 4 * (n + 1))
                A_.done(e.activation(vh[:, bass.ds(n, 1), :].rearrange("p o t -> p (o t)"), MB[:, :],
                                     ACT.Identity, bias=mcol(3, n), scale=mcol(4, n)), "h2T_keep")
            steps.append({"dve": norm, "pe": turn, "act": modulate})

            for half in range(2):
                def route(e, half=half):
                    A_.wait(e, "h2T_keep" if half == 0 else "log0", n)
                    for k in range(2):
                        t = 2 * half + k
                        e.matmul(MB[:, k * NE:(k + 1) * NE], ones_row[:, :], eb_row[:, :], start=True, stop=False)
                        last = e.matmul(MB[:, k * NE:(k + 1) * NE], h2T[:, t * P:(t + 1) * P], col["rw"],
                                        start=False, stop=True)
                    P_.done(last, f"log{half}")

                def route_keep(e, half=half):
                    P_.wait(e, f"log{half}", n)
                    if half == 0:
                        D_.wait(e, "cut", n - 1)
                    A_.done(e.activation(logit[:, 2 * half:2 * half + 2, :],
                                         MB[:, 0:2 * NE].rearrange("p (t k) -> p t k", k=NE), ACT.Identity),
                            f"log{half}")
                steps.append({"pe": route, "act": route_keep})

            def top(e):
                A_.wait(e, "log1", n)
                apart(e)
                for t in range(NT):
                    last = e.max(v8[:, t, :], logit[:, t, :])
                D_.done(last, "v8")
                D_.wait(e, "v8", n)
                apart(e)
                for t in range(NT):
                    last = e.max_index(i8[:, t, :], v8[:, t, :], logit[:, t, :])
                D_.done(last, "i8")

            def cut(e):
                for t in range(NT):
                    last = e.match_replace(logit_cut[:, t, :], v8[:, t, :], logit[:, t, :], NEG)
                D_.done(last, "cut")
                D_.wait(e, "cut", n)
                P_.wait(e, "z1", n - 1)
                D_.done(e.tensor_scalar(chosen[:, :, :], logit_cut[:, :, :], NEG, None, ALU.is_equal), "chosen")
                D_.done(e.tensor_copy(i8f[:, :, :], i8[:, :, :]), "i8f")
                D_.done(e.tensor_copy(v8_all[:, bass.ds(n * NT * TOPK, NT * TOPK)],
                                      v8[:, :, :].rearrange("p t k -> p (t k)")), "v8_keep")

            def count(e):
                D_.wait(e, "chosen", n)
                for t in range(NT):
                    last = e.matmul(MB[0:1, 0:NE], onesb[:, 0:1], chosen[:, t, :], start=(t == 0), stop=(t == NT - 1))
                P_.done(last, "cnt")
            steps.append({"dve": top})
            steps.append({"dve": cut, "pe": count})

            paging = (
                ("total", lambda e: e.tensor_tensor(total[:, :], fill[:, :], MB[0:1, 0:NE], ALU.add)),
                ("total_i", lambda e: e.tensor_scalar(total_i[:, :], total[:, :], float(P - 1), None, ALU.add)),
                ("full_i", lambda e: e.tensor_scalar(full_i[:, :], total_i[:, :], 7, None, ALU.logical_shift_right)),
                ("newp", lambda e: e.tensor_scalar(newp[:, :], full_i[:, :], -1.0, 0.0, ALU.add, ALU.max)),
                ("endp", lambda e: e.tensor_tensor_scan(endp[:, :], newp[:, :], zero_row[:, :], nextp[:, :],
                                                        ALU.add, ALU.add)),
                ("curd0", lambda e: e.tensor_tensor(curd[:, :], endp[:, :], newp[:, :], ALU.subtract)),
                ("jump0", lambda e: e.tensor_tensor(rows[:, 0, :], curd[:, :], cur[:, :], ALU.subtract)),
                ("jump", lambda e: e.tensor_scalar(rows[:, 0, :], rows[:, 0, :], float(P), -float(P), ALU.mult, ALU.add)),
                ("openrow", lambda e: e.tensor_scalar(rows[:, 1, :], cur[:, :], float(P), float(P), ALU.mult, ALU.add)),
                ("filled", lambda e: e.tensor_scalar(rows[:, 2, :], fill[:, :], -float(P), None, ALU.add)),
                ("fill", lambda e: e.scalar_tensor_tensor(out=fill[:, :], in0=newp[:, :], scalar=-float(P),
                                                          in1=total[:, :], op0=ALU.mult, op1=ALU.add)),
                ("curd1", lambda e: e.scalar_tensor_tensor(out=curd[:, :], in0=endp[:, :], scalar=-1.0, in1=cur[:, :],
                                                           op0=ALU.add, op1=ALU.subtract)),
                ("curd2", lambda e: e.scalar_tensor_tensor(out=curd[:, :], in0=newp[:, :], scalar=0.0, in1=curd[:, :],
                                                           op0=ALU.is_gt, op1=ALU.mult)),
                ("cur", lambda e: e.tensor_tensor(cur[:, :], cur[:, :], curd[:, :], ALU.add)),
                ("nextp", lambda e: e.tensor_copy(nextp[:, :], endp[:, NE - 1:NE])))

            def page_op(e, k):
                name, f = paging[k]
                if k == 0:
                    P_.wait(e, "cnt", n)
                elif name not in ("openrow", "filled"):
                    D_.wait(e, paging[k - 1][0], n)
                if name == "endp":
                    wait(e, s_ends, 16 * n)
                if name == "jump0":
                    P_.wait(e, "z1", n - 1)
                D_.done(f(e), name)

            def spread(e):
                D_.wait(e, "filled", n)
                P_.done(e.matmul(MB[:, 0:2 * NE], ones_row[:, :], rows[:, 0:2, :].rearrange("p a k -> p (a k)"),
                                 start=True, stop=True), "bc")

            def spread_keep(e):
                P_.wait(e, "bc", n)
                D_.wait(e, "place1", n - 1)
                A_.done(e.activation(page_bc[:, :, :].rearrange("p a k -> p (a k)"), MB[:, 0:2 * NE],
                                     ACT.Identity), "bc")
            def ends_store(e):
                D_.wait(e, "endp", n)
                e.dma_start(ends_d[:, bass.ds(n * NE, NE)], endp[:, :]).then_inc(s_ends, 16)
            for k in range(0, len(paging), 3):
                steps.append({"dve": lambda e, k=k: [page_op(e, kk) for kk in range(k, min(k + 3, len(paging)))]})
            steps.append({"pe": spread, "act": spread_keep, "sp": ends_store})

            for half in range(2):
                def rank(e, half=half):
                    if half == 0:
                        A_.wait(e, "bc", n)
                    else:
                        D_.wait(e, "zs0", n)
                    for k in range(2):
                        dst = MB[:, k * NE:(k + 1) * NE]
                        e.matmul(dst, ones_row[:, :], rows[:, 2, :], start=True, stop=False)
                        for t in range(2 * half + k):
                            e.matmul(dst, onesb, chosen[:, t, :], start=False, stop=False)
                        last = e.matmul(dst, upper, chosen[:, 2 * half + k, :], start=False, stop=True)
                    P_.done(last, f"z{half}")

                def where(e, half=half):
                    z = MB[:, 0:2 * NE].rearrange("p (t k) -> p t k", k=NE)
                    wide = [page_bc[:, a:a + 1, :].broadcast_to([P, 2, NE]) for a in range(2)]
                    P_.wait(e, f"z{half}", n)
                    A_.wait(e, "bc", n)
                    D_.done(e.scalar_tensor_tensor(out=step_p[:, :, :], in0=z, scalar=0.0, in1=wide[0],
                                                   op0=ALU.is_ge, op1=ALU.mult), f"step{half}")
                    if half == 1:
                        D_.wait(e, "pos0", n)
                    D_.done(e.tensor_tensor(place[:, :, :], z, wide[1], ALU.add), f"zs{half}")
                    D_.wait(e, f"zs{half}", n)
                    D_.done(e.tensor_tensor(place[:, :, :], place[:, :, :], step_p[:, :, :], ALU.add), f"place{half}")

                def pick(e, half=half, k=0, part_=0):
                    if part_ == 0:
                        D_.wait(e, f"place{half}" if k == 0 else f"pick{half}", n)
                    for kk in range(4 * part_, 4 * part_ + 4):
                        last = e.scalar_tensor_tensor(out=junk[:, kk, :], in0=iota_e,
                                                      scalar=i8f[:, 2 * half + k, kk:kk + 1], in1=place[:, k, :],
                                                      op0=ALU.is_equal, op1=ALU.mult,
                                                      accum_out=pos8[:, 2 * half + k, kk:kk + 1])
                    if part_:
                        D_.done(last, f"pos{half}" if k else f"pick{half}")
                steps.append({"pe": rank, "dve": where})
                for k in range(2):
                    for part_ in range(2):
                        steps.append({"dve": lambda e, pick=pick, k=k, part_=part_: pick(e, k=k, part_=part_)})

            def back(e):
                D_.wait(e, "zs1", n)
                for t in range(NT):
                    last = e.transpose(MB[:, t * P:(t + 1) * P], h2T[:, t * P:(t + 1) * P], ident)
                P_.done(last, "h2")

            def back_keep(e):
                P_.wait(e, "h2", n)
                wait(e, s_scat, 16 * NT * TOPK * n)
                A_.done(e.activation(h2[:, :, :].rearrange("p t d -> p (t d)"), MB[:, :], ACT.Identity), "h2")
            steps.append({"pe": back, "act": back_keep})

            def keep(e):
                D_.wait(e, "pos1", n)
                wait(e, s_scat, 16 * NT * TOPK * n)
                D_.done(e.tensor_copy(pos_s[:, :], pos8[:, :, :].rearrange("p t k -> p (t k)")), "pos_s")
                D_.done(e.tensor_copy(pos_all[:, bass.ds(n * NT, NT), :], pos8[:, :, :]), "pos_keep")

            steps.append({"dve": keep})
            return steps

        def scatters(n):
            return [{"pool": lambda e, t=t, k=k: scatter(e, n, t, k)} for t in range(NT) for k in range(TOPK)]

        def turn_a(i, ex_=True, pre_=True, mx_=True, post_=True, scat_=True):
            streams = []
            if ex_:
                streams.append((ex(i), 0.0, 0.97, 0.95))
                streams.append((exp_loads(i, (2,)), 0.27, 0.27))
                streams.append((exp_loads(i, (3,)), 0.52, 0.52))
            if mx_:
                streams.append((mx(i + 1), 0.0, 0.88, 0.95))
                streams.append((exp_loads(i + 1, (0, 1)), 0.96, 1.0))
            if pre_:
                streams.append((pre(i + 2), 0.0, 0.85))
                streams.append((max_loads(i + 2, (0, 1)), 0.9, 0.92))
            if post_:
                streams.append((post(i - 1), 0.0, 0.97))
            if scat_:
                streams.append((scatters(i - 2), 0.0, 0.8))
            return merge(*streams)

        small = sb("small", [P, 4, PCOL])
        tab = qm[0:1, :, :, :].rearrange("p a h t -> p (a h t)").bitcast(I32)[:, 0:PCOL * P]
        table_i = sb("table_i", [P, PCOL], I32)
        arena = prob[:, :, :].rearrange("p a b -> p (a b)")
        ends_bc = arena[:, 0:NB * NE]
        ends_junk = arena[:, NB * NE:4 * NB * NE].bitcast(BF16).rearrange("p (c e) -> p c e", c=PCOL)
        gb_bc = arena[:, 4 * GRP * WROW:4 * GRP * WROW + NB * D].rearrange("p (n d) -> p n d", d=D)
        x_in = v_ext[:, :, :, :].rearrange("p t h d -> p (t h d)").rearrange("p (g r) -> p g r", g=4)
        w_in = arena[:, 0:4 * GRP * WROW].rearrange("p (g j w) -> p g j w", g=4, j=GRP)
        o_ = 2 * NB * NE
        x_T = [arena[:, o_ + i * 512:o_ + (i + 1) * 512] for i in range(2)]
        h_g = [arena[:, o_ + 1024 + i * 256:o_ + 1024 + (i + 1) * 256] for i in range(2)]
        y_sb = [arena[:, o_ + 1536 + i * 512:o_ + 1536 + (i + 1) * 512] for i in range(4)]
        s_xl = [sem(f"s_xl{g}") for g in range(4)]
        s_ys = [sem(f"s_ys{g}") for g in range(4)]
        s_T, s_XT, s_G, s_H, s_Y, s_YD, s_YA = (sem(n) for n in ("s_T", "s_XT", "s_G", "s_H", "s_Y", "s_YD", "s_YA"))

        LAST = NB - 1
        table = [
            {"sp": lambda e: [
                e.wait_ge(s_ends, 16 * NB),
                wait(e, s_pv, 4 * NB),
                e.dma_start(ends_bc, ends_d[0, :].partition_broadcast(P)).then_inc(s_tab, 16)]},
            {"dve": lambda e: [
                e.wait_ge(s_tab, 16),
                post_d.wait(e, "pos_keep", LAST),
                [e.tensor_scalar(ends_junk[:, c, :], ends_bc, page_no[:, c:c + 1], 0.0, ALU.is_le, ALU.add,
                                 accum_out=small[:, 0, c:c + 1]) for c in range(PCOL)],
                [e.tensor_scalar(junk[:, c, 0:NB], ends_bc.rearrange("p (n k) -> p n k", k=NE)[:, :, NE - 1],
                                 page_no[:, c:c + 1], 0.0, ALU.is_le, ALU.add,
                                 accum_out=small[:, 1, c:c + 1]) for c in range(PCOL)][-1].then_inc(s_tabd, 1),
                e.wait_ge(s_tabd, 1),
                e.scalar_tensor_tensor(out=small[:, 2, :], in0=small[:, 1, :], scalar=-float(NE), in1=small[:, 0, :],
                                       op0=ALU.mult, op1=ALU.add).then_inc(s_tabd, 1),
                e.tensor_scalar(small[:, 3, :], page_no, float(NE), None, ALU.is_lt).then_inc(s_tabd, 1),
                e.wait_ge(s_tabd, 3),
                e.tensor_tensor(small[:, 0, :], page_no, small[:, 2, :], ALU.subtract).then_inc(s_tabd, 1),
                e.wait_ge(s_tabd, 4),
                e.tensor_tensor(small[:, 0, :], small[:, 0, :], small[:, 3, :], ALU.mult).then_inc(s_tabd, 1),
                e.wait_ge(s_tabd, 5),
                e.tensor_tensor(small[:, 0, :], small[:, 0, :], small[:, 2, :], ALU.add).then_inc(s_tabd, 1),
                e.wait_ge(s_tabd, 6),
                e.tensor_scalar(table_i[:, :], small[:, 0, :], float(P), None, ALU.mult).then_inc(s_tabd, 1)]},
            {"sp": lambda e: [
                e.wait_ge(s_tabd, 7),
                e.dma_start(table_d.rearrange("(c p) -> p c", p=P), table_i[:, :],
                            allow_slow_non_contiguous=True).then_inc(s_tab, 16),
                e.wait_ge(s_tab, 32),
                e.dma_start(tab[:, :], table_d.rearrange("(o c) -> o c", o=1)).then_inc(s_tab, 16),
                e.wait_ge(s_tab, 48),
                e.wait_ge(s_scat, 16 * NT * TOPK * NB)]},
        ]

        TX, GT, YP = bank[0:2], bank[2:4], [bank[4:6], bank[6:8]]

        def b_group(k, g):
            return 4 * k + g

        def b_rows(G):
            return pages[bass.ds(G * GRP * P, GRP * P), :].rearrange("(j p) d -> p j d", p=P)

        def b_load(k):
            def f(e):
                _, wrow = nc.values_load_multi_w_load_instructions(
                    tab[0:1, bass.ds(k * 4 * GRP, 4 * GRP)], engines=[mybir.EngineType.SP],
                    min_val=0, max_val=(NE - 1) * P)
                for g in range(4):
                    G = b_group(k, g)
                    wait(e, s_Y, G - 3)
                    e.dma_start(x_in[:, g, :].rearrange("p (j d) -> p j d", d=D), b_rows(G)).then_inc(s_xl[g], 16)
                    for j in range(GRP):
                        e.dma_start(w_in[:, g, j, :], wexp[bass.ds(wrow[g * GRP + j], P), :]).then_inc(s_xl[g], 16)
                    if not isinstance(k, int) or k > 0:
                        b_store(e, G - 4, g)
            return {"sp": f}

        def b_store(e, G, g):
            wait(e, s_YD, G + 1)
            wait(e, s_YA, G + 1)
            e.dma_start(b_rows(G), y_sb[g].rearrange("p (j d) -> p j d", d=D)).then_inc(s_ys[g], 16)

        XL = 16 * (GRP + 1)

        def b_steps(k, which):
            steps = []
            for g in which:
                G = b_group(k, g)
                first = isinstance(k, int) and k == 0

                def tr(e, G=G, g=g):
                    e.wait_ge(s_xl[g], XL * (k + 1))
                    wait(e, s_XT, G - 1)
                    for j in range(GRP):
                        last = e.transpose(TX[g % 2][:, j * P:(j + 1) * P], x_in[:, g, j * D:(j + 1) * D], ident)
                    last.then_inc(s_T, 1)

                def xt(e, G=G, g=g):
                    e.wait_ge(s_T, G + 1)
                    wait(e, s_G, G - 1)
                    e.tensor_copy(x_T[g % 2], TX[g % 2][:, :]).then_inc(s_XT, 1)

                def gate(e, G=G - 1, g=(g - 1) % 4):
                    e.wait_ge(s_XT, G + 1)
                    wait(e, s_H, G - 1)
                    for j in range(GRP):
                        half = 64 * (j % 2)
                        last = e.matmul(GT[g % 2][half:half + 64, (j // 2) * P:(j // 2 + 1) * P],
                                        w_in[:, g, j, 0:INTER], x_T[g % 2][:, j * P:(j + 1) * P],
                                        start=True, stop=True)
                    last.then_inc(s_G, 1)

                def silu(e, G=G - 1, g=(g - 1) % 4):
                    e.wait_ge(s_G, G + 1)
                    wait(e, s_Y, G - 1)
                    e.activation(h_g[g % 2], GT[g % 2][:, 0:2 * P], ACT.Silu).then_inc(s_H, 1)

                def down(e, G=G - 2, g=(g - 2) % 4):
                    e.wait_ge(s_H, G + 1)
                    wait(e, s_YD, G - 1)
                    wait(e, s_YA, G - 1)
                    for j in range(GRP):
                        half = 64 * (j % 2)
                        last = e.matmul(YP[g % 2][j % 2][:, (j // 2) * D:(j // 2 + 1) * D],
                                        h_g[g % 2][half:half + 64, (j // 2) * P:(j // 2 + 1) * P],
                                        w_in[half:half + 64, g, j, INTER:WROW], start=True, stop=True)
                    last.then_inc(s_Y, 1)

                def y_out(e, par, s_mine, G=G - 2, g=(g - 2) % 4, stores=k if g >= 2 else k - 1):
                    e.wait_ge(s_Y, G + 1)
                    wait(e, s_ys[g], 16 * stores)
                    dst = y_sb[g].rearrange("p (j a d) -> p j a d", a=2, d=D)[:, :, par, :]
                    src = YP[g % 2][par][:, 0:2 * D].rearrange("p (j d) -> p j d", d=D)
                    if par == 0:
                        e.tensor_copy(dst, src).then_inc(s_mine, 1)
                    else:
                        e.activation(dst, src, ACT.Identity).then_inc(s_mine, 1)
                step = {}
                pe, dve, act = [], [], []
                end = isinstance(k, int) and k == NGRP // 4
                if not end:
                    pe.append(tr)
                    dve.append(xt)
                if not (first and g < 1) and not (end and g > 0):
                    pe.append(gate)
                    act.append(silu)
                if not (first and g < 2):
                    pe.append(down)
                    dve.append(lambda e, f=y_out: f(e, 0, s_YD))
                    act.append(lambda e, f=y_out: f(e, 1, s_YA))
                for name, fs in (("pe", pe), ("dve", dve), ("act", act)):
                    step[name] = lambda e, fs=fs: [f(e) for f in fs]
                steps.append(step)
            return steps

        w8 = v8_all
        wsum = sb("wsum", [P, NB * NT])
        pos_g = sb("pos_g", [P, 2, TOPK], U32)
        yg = [b[:, :, :, :].rearrange("p a h t -> p (a h t)").bitcast(F32).rearrange("p (k d) -> p k d", d=D)
              for b in (qe, ke)]
        acc, o_sb = onorm[:, 0:2, :], onorm[:, 2:4, :]
        hs = att[0:INTER, :]
        s_w8a, s_w8d, s_gbd, s_gbp, s_gba = (sem(n) for n in ("s_w8a", "s_w8d", "s_gbd", "s_gbp", "s_gba"))
        s_pg, s_acc, s_fin, s_shp, s_sha, s_shd = (sem(n) for n in ("s_pg", "s_acc", "s_fin", "s_shp", "s_sha", "s_shd"))
        s_yg = [sem("s_yg0"), sem("s_yg1")]
        s_o = [sem("s_o0"), sem("s_o1")]

        weigh = [
            {"act": lambda e: [post_d.wait(e, "v8_keep", LAST),
                               e.activation(w8[:, :], v8_all[:, :], ACT.Exp, scale=-1.0).then_inc(s_w8a, 1)]},
            {"dve": lambda e: [
                e.wait_ge(s_w8a, 1),
                e.tensor_scalar(w8[:, :], w8[:, :], 1.0, None, ALU.add).then_inc(s_w8d, 1), e.wait_ge(s_w8d, 1),
                e.reciprocal(w8[:, :], w8[:, :]).then_inc(s_w8d, 1), e.wait_ge(s_w8d, 2),
                e.tensor_reduce(wsum[:, :], w8[:, :].rearrange("p (t k) -> p t k", k=TOPK), AX.X, ALU.add)
                 .then_inc(s_w8d, 1), e.wait_ge(s_w8d, 3),
                e.tensor_scalar(wsum[:, :], wsum[:, :], 1e-9, None, ALU.add).then_inc(s_w8d, 1), e.wait_ge(s_w8d, 4),
                e.reciprocal(wsum[:, :], wsum[:, :]).then_inc(s_w8d, 1), e.wait_ge(s_w8d, 5),
                e.tensor_tensor(w8[:, :].rearrange("p (t k) -> p t k", k=TOPK),
                                w8[:, :].rearrange("p (t k) -> p t k", k=TOPK),
                                wsum[:, :].rearrange("p (t o) -> p t o", o=1).broadcast_to([P, NB * NT, TOPK]),
                                ALU.mult).then_inc(s_w8d, 1), e.wait_ge(s_w8d, 6),
                e.tensor_scalar(w8[:, :], w8[:, :], 2.5, None, ALU.mult).then_inc(s_w8d, 1)]},
        ]

        ones_sq = sb("ones_sq", [P, P])
        diag4 = x_in[:, 0, :].rearrange("p (a d) -> p a d", a=4)

        def gates():
            steps = [{"dve": lambda e: [e.wait_ge(s_YD, NGRP), e.memset(ones_sq[:, :], 1.0).then_inc(s_gbd, 1)]}]
            for q in range(4):
                def dg(e, q=q):
                    if q:
                        e.wait_ge(s_gbp, q)
                    for a in range(4):
                        last = e.tensor_scalar(diag4[:, a, :], ident, mod[:, 5, 4 * q + a:4 * q + a + 1], None, ALU.mult)
                    last.then_inc(s_gbd, 1)

                def mm(e, q=q):
                    e.wait_ge(s_gbd, q + 2)
                    e.wait_ge(s_YA, NGRP)
                    if q:
                        e.wait_ge(s_gba, q)
                    e.matmul(bank[7][:, :], ones_sq[:, :], diag4.rearrange("p a d -> p (a d)"),
                             start=True, stop=True).then_inc(s_gbp, 1)

                def take(e, q=q):
                    e.wait_ge(s_gbp, q + 1)
                    e.activation(gb_bc[:, 4 * q:4 * q + 4, :].rearrange("p a d -> p (a d)"), bank[7][:, :],
                                 ACT.Identity).then_inc(s_gba, 1)
                steps.append({"dve": dg, "pe": mm, "act": take})
            return steps

        def final(n):
            steps = []

            def up(e):
                wait(e, s_sha, n)
                e.matmul(bank[0][0:INTER, :], col["wgs"], vh[:, bass.ds(n, 1), :].rearrange("p o t -> p (o t)"),
                         start=True, stop=True).then_inc(s_shp, 1)

            def act(e):
                e.wait_ge(s_shp, 2 * n + 1)
                e.activation(hs, bank[0][0:INTER, :], ACT.Silu).then_inc(s_sha, 1)

            def down(e):
                e.wait_ge(s_sha, n + 1)
                wait(e, s_fin, NT * n)
                for t in range(NT):
                    last = e.matmul(bank[1][:, t * D:(t + 1) * D], hs[:, t * P:(t + 1) * P], wds_sb[:, :],
                                    start=True, stop=True)
                last.then_inc(s_shp, 1)
            steps.append({"pe": lambda e: [up(e), down(e)], "act": act})
            for t in range(NT):
                T_, b = n * NT + t, t % 2

                def gather(e, T_=T_, b=b):
                    e.wait_ge(s_pg, T_ + 1)
                    wait(e, s_acc, TOPK * (T_ - 1))
                    apart(e)
                    for k in range(TOPK):
                        e.indirect_dma_start(out=yg[b][:, k, :], out_offset=None, in_=pages,
                                             in_offset=bass.IndirectOffsetOnAxis(ap=pos_g[:, b, k:k + 1], axis=0)) \
                         .then_inc(s_yg[b], 16)

                def places(e, T_=T_, b=b, t=t):
                    e.tensor_copy(pos_g[:, b, :], pos_all[:, bass.ds(T_, 1), :].rearrange("p o k -> p (o k)")) \
                     .then_inc(s_pg, 1)

                def combine(e, T_=T_, b=b, t=t):
                    e.wait_ge(s_yg[b], 16 * TOPK * (2 * n + t // 2 + 1))
                    wait(e, s_fin, T_ - 1)
                    if t == 0:
                        e.wait_ge(s_shp, 2 * n + 2)
                    wcol = w8[:, bass.ds(T_ * TOPK, TOPK)]
                    for k in range(TOPK):
                        e.scalar_tensor_tensor(
                            out=acc[:, b, :], in0=yg[b][:, k, :], scalar=wcol[:, k:k + 1],
                            in1=bank[1][:, t * D:(t + 1) * D] if k == 0 else acc[:, b, :],
                            op0=ALU.mult, op1=ALU.add).then_inc(s_acc, 1)
                        e.wait_ge(s_acc, TOPK * T_ + k + 1)
                    e.tensor_tensor(acc[:, b, :], acc[:, b, :],
                                    gb_bc[:, bass.ds(n, 1), :].rearrange("p o d -> p (o d)"), ALU.mult) \
                     .then_inc(s_shd, 1)
                    e.wait_ge(s_shd, T_ + 1)
                    wait(e, s_o[b], 16 * (2 * n + t // 2))
                    e.tensor_tensor(o_sb[:, b, :], acc[:, b, :], xtile(n, t), ALU.add).then_inc(s_fin, 1)

                def put(e, T_=T_, b=b, t=t):
                    wait(e, s_fin, T_ + 1)
                    e.dma_start(out[bass.ds(n, 1), t * P:(t + 1) * P, :].rearrange("o p d -> (o p) d"),
                                o_sb[:, b, :]).then_inc(s_o[b], 16)
                steps.append((gather, places, combine, put))
            return steps

        def stage_c(e, name):
            def tile(n, t):
                s_ = final(n)
                if name == "pool":
                    s_[1 + t][0](e)
                if name == "dve":
                    s_[1 + t][2](e)
                    n2, t2 = (n, t + 2) if t < 2 else (n + 1, t - 2)
                    if not (isinstance(n2, int) and n2 == NB):
                        final(n2)[1 + t2][1](e)
                if name == "sp":
                    s_[1 + t][3](e)

            def round_(n):
                run(name, e, final(n)[0:1])
                for t in range(NT):
                    tile(n, t)
            if name == "dve":
                e.wait_ge(s_tab, 48)
                final(0)[1][1](e)
                final(0)[2][1](e)
                e.wait_ge(s_w8d, 7)
                e.wait_ge(s_gba, 4)
            if name == "pool":
                for g in range(4):
                    e.wait_ge(s_ys[g], 16 * NGRP // 4)
            round_(0)
            with e.Fori(1, NB - 1) as n:
                round_(n)
            round_(NB - 1)
            if name == "sp":
                for b in range(2):
                    e.wait_ge(s_o[b], 16 * NB * NT // 2)

        def program(name):
            def f(e):
                run(name, e, setup)
                run(name, e, turn_a(-2, ex_=False, mx_=False, post_=False, scat_=False))
                run(name, e, turn_a(-1, ex_=False, post_=False, scat_=False))
                run(name, e, turn_a(0, post_=False, scat_=False))
                run(name, e, turn_a(1, scat_=False))
                with e.Fori(2, NB - 2) as i:
                    run(name, e, turn_a(i))
                run(name, e, turn_a(NB - 2, pre_=False))
                run(name, e, turn_a(NB - 1, pre_=False, mx_=False))
                run(name, e, merge((post(NB - 1), 0.0, 1.0), (scatters(NB - 2), 0.0, 0.8)))
                run(name, e, scatters(NB - 1))
                run(name, e, weigh + table)
                if name == "sp":
                    run(name, e, [b_load(0)])
                    with e.Fori(1, NGRP // 4) as k:
                        run(name, e, [b_load(k)])
                    for g in range(4):
                        b_store(e, NGRP - 4 + g, g)
                if name in ("pe", "dve", "act"):
                    if name == "pe":
                        e.wait_ge(s_tabd, 7)
                        post_d.wait(e, "zs1", LAST)
                        pre_d.wait(e, "v", LAST)
                    if name in ("dve", "act"):
                        e.wait_ge(s_tabd, 7)
                    run(name, e, b_steps(0, range(4)))
                    with e.Fori(1, NGRP // 4) as k:
                        run(name, e, b_steps(k, range(4)))
                    run(name, e, b_steps(NGRP // 4, range(2)))
                run(name, e, gates())
                stage_c(e, name)
            return f

        block = ctx.enter_context(nc.Block())
        block.sync(program("sp"))
        block.gpsimd(program("pool"))
        block.tensor(program("pe"))
        block.vector(program("dve"))
        block.scalar(program("act"))


def kernel(L0_attn_x, L0_attn_qkv_w, L0_attn_qkv_b, L0_attn_proj_w, L0_attn_proj_b, L0_ffn_router_w,
           L0_ffn_expert_bias, L0_ffn_w_gate, L0_ffn_w_down, L0_ffn_w_gate_shared, L0_ffn_w_down_shared,
           L0_c, L0_wmod):
    import ml_dtypes
    import numpy as np
    import concourse.bacc as bacc
    from concourse.bass_utils import run_bass_kernel_spmd

    a = lambda v: np.asarray(v)
    qkv_w, qkv_b = a(L0_attn_qkv_w), a(L0_attn_qkv_b)
    h2, par, d = np.arange(8), np.arange(2), np.arange(HD)
    order = ((2 * h2[None, None, :] + par[:, None, None]) * HD + d[None, :, None]).reshape(-1)
    turned = ((2 * h2[None, None, :] + par[:, None, None]) * HD + ((d + HD // 2) % HD)[None, :, None]).reshape(-1)
    wq, wk, wv = qkv_w[0:D], qkv_w[D:2 * D], qkv_w[2 * D:3 * D]
    bq, bk, bv = qkv_b[0:D], qkv_b[D:2 * D], qkv_b[2 * D:3 * D]
    wts = np.concatenate([
        wq[order].T, wq[turned].T, wk[order].T, wk[turned].T, wv.T, a(L0_attn_proj_w).T, a(L0_ffn_router_w).T,
        a(L0_wmod), a(L0_c).T, a(L0_ffn_w_gate_shared).T, bq[order][:, None], bq[turned][:, None],
        bk[order][:, None], bk[turned][:, None], a(L0_attn_proj_b)[:, None]], axis=1)
    wg, wd = a(L0_ffn_w_gate).transpose(0, 2, 1), a(L0_ffn_w_down).transpose(0, 2, 1)
    wexp = np.concatenate([wg, np.concatenate([wd, wd], axis=1)], axis=2).reshape(NE * P, WROW)

    freqs = (1.0 / 10000.0 ** (np.arange(HD // 2, dtype=np.float32) / np.float32(HD // 2))).astype(np.float32)
    angle = np.arange(S, dtype=np.float32)[:, None] * freqs[None, :]
    dd = order % HD
    cos = np.cos(angle).astype(np.float32).T[dd % (HD // 2)]
    sin = np.sin(angle).astype(np.float32).T[dd % (HD // 2)] * np.where(dd < HD // 2, -1.0, 1.0)[:, None]
    page_no = np.arange(PCOL)[None, :] * P + np.arange(P)[:, None]
    const = np.concatenate([cos, sin, np.eye(P), np.tile(np.arange(NE), (P, 1)), page_no], axis=1).astype(np.float32)
    r, c = np.arange(P)[:, None], np.arange(P)[None, :]
    constb = np.concatenate([np.where(c > r, -1e9, 0.0), np.where(r > c, -1e9, 0.0), np.eye(P), r < c,
                             np.ones((P, P))], axis=1).astype(ml_dtypes.bfloat16)
    arrays = {"x": a(L0_attn_x), "wts": wts, "bvec": bv, "brow": a(L0_ffn_expert_bias)[None, :],
              "wexp": wexp, "wds": a(L0_ffn_w_down_shared).T, "const": const, "constb": constb}
    arrays = {k: np.ascontiguousarray(v) for k, v in arrays.items()}
    nc = bacc.Bacc("TRN2", target_bir_lowering=False, num_devices=1)
    ins = [nc.dram_tensor(k, v.shape, mybir.dt.from_np(v.dtype), kind="ExternalInput").ap()
           for k, v in arrays.items()]
    out = nc.dram_tensor("out", (NB, S, D), F32, kind="ExternalOutput").ap()
    build(nc, *ins, out)
    return run_bass_kernel_spmd(nc, [arrays], core_ids=[0]).results[0]["out"]
```

```python
from contextlib import ExitStack

import concourse.bass as bass
import concourse.mybir as mybir
from concourse.alu_op_type import AluOpType as ALU

F32, BF16, I32, U32 = mybir.dt.float32, mybir.dt.bfloat16, mybir.dt.int32, mybir.dt.uint32
ACT = mybir.ActivationFunctionType
AX = mybir.AxisListType

P = 128
NB, S, D = 16, 512, 128
NT = S // P
H, HD = 16, 8
NE, TOPK, INTER = 160, 8, 64
NPAGE = NE + NB * S * TOPK // P
GRP = 4
NGRP = NPAGE // GRP
PCOL = -(-NPAGE // P)
SLOTS = 8
MAXROW = 48
Q_RUNS = ((0, (0, 0, 0)), (3, (1, 1)), (5, (2,)))
K_RUNS = ((0, (0, 1, 2)), (3, (0, 1)), (5, (0,)))
EPS = 1e-5
SCALE = 1.0 / HD ** 0.5
NEG = -3.0e38
WROW = INTER + D
BASE, IDS, WTS = D, D + 1, D + 1 + TOPK
ROW = WTS + TOPK
FREE_SETS = 3
TAKEN = float(2 ** 18)
FREE = FREE_SETS * GRP * P


class Events:

    def __init__(self, sem, names):
        self.sem, self.names, self.k = sem, names, 0

    def done(self, ins, name):
        assert self.names[self.k % len(self.names)] == name, (name, self.names[self.k % len(self.names)])
        self.k += 1
        ins.then_inc(self.sem, 1)

    def wait(self, eng, name, n):
        wait(eng, self.sem, n * len(self.names) + self.names.index(name) + 1)


def wait(eng, sem, value):
    if not isinstance(value, int) or value > 0:
        eng.wait_ge(sem, value)
    if not isinstance(value, int) and eng.engine == mybir.EngineType.SP:
        apart(eng)


def apart(eng):
    eng.nop(nofuse=True)


def merge(*streams):
    timed = []
    for order, (steps, start, end, *lag) in enumerate(streams):
        share = (end - start) / len(steps)
        for k, step in enumerate(steps):
            for j, (name, f) in enumerate(step.items()):
                at = start + share * (k + 0.5 + j * (lag[0] if lag else 0.9) / max(len(step) - 1, 1))
                timed.append((at, order, k, j, {name: f}))
    return [t[-1] for t in sorted(timed, key=lambda t: t[:4])]


def run(eng_name, eng, steps):
    for step in steps:
        if eng_name in step:
            step[eng_name](eng)


def build(nc, x, wts, bvec, brow, wexp, wds, const, constb, out):
    with ExitStack() as ctx:
        def sb(name, shape, dt=F32):
            return ctx.enter_context(nc.sbuf_tensor(name, shape, dt))

        def sem(name):
            return ctx.enter_context(nc.semaphore(name))

        qd = nc.dram_tensor("q_stacks", (NB, 2, 64, 8 * S), BF16, kind="Internal").ap()
        kd = nc.dram_tensor("k_stacks", (NB, 2, 64, 8 * S), BF16, kind="Internal").ap()
        pages = nc.dram_tensor("pages", (NPAGE * P, ROW), F32, kind="Internal").ap()
        results = nc.dram_tensor("results", (NB * S * TOPK + FREE, D), F32, kind="Internal").ap()
        ends_d = nc.dram_tensor("page_ends", (1, NB * NE), F32, kind="Internal").ap()
        table_d = nc.dram_tensor("page_table", (PCOL * P,), I32, kind="Internal").ap()

        nw = wts.shape[1]
        w_all = sb("w_all", [P, nw])
        col = {}
        at = 0
        for name, width in (("wq", D), ("wqr", D), ("wk", D), ("wkr", D), ("wv", D), ("wp", D), ("rw", NE),
                            ("wmod", 6 * D), ("cT", NB), ("wgs", INTER), ("bq", 1), ("bqr", 1), ("bk", 1),
                            ("bkr", 1), ("bp", 1)):
            col[name] = w_all[:, at:at + width]
            at += width
        assert at == nw
        bv_bc = sb("bv_bc", [P, D])
        eb_row = sb("eb_row", [1, NE])
        wds_sb = sb("wds_sb", [INTER, D])
        c_all = sb("c_all", [P, const.shape[1]])
        cosT, sinT = c_all[:, 0:S], c_all[:, S:2 * S]
        ident = c_all[:, 2 * S:2 * S + P]
        iota_e = c_all[:, 2 * S + P:2 * S + P + NE]
        page_no = c_all[:, 2 * S + P + NE:2 * S + P + NE + PCOL]
        o_ = 2 * S + P + NE + PCOL
        row_0, row_free = c_all[:, o_:o_ + NT], c_all[:, o_ + NT:o_ + NT + GRP]
        cb_all = sb("cb_all", [P, 5 * P], BF16)
        mask_q, mask_k, identb, upper, onesb = (cb_all[:, i * P:(i + 1) * P] for i in range(5))
        ones_row = sb("ones_row", [1, P])
        zero_row = sb("zero_row", [1, NE])
        zerob = sb("zerob", [P, S], BF16)
        oneb = sb("oneb", [P, S], BF16)
        mhalf = sb("mhalf", [P, NT])
        silu_c = sb("silu_c", [P, NB])
        sig_c = sb("sig_c", [P, NB])
        mod = sb("mod", [P, 6, NB])
        gsign = sb("gsign", [P, 2, NB])
        gabs = sb("gabs", [P, 2, NB])
        gneg = sb("gneg", [P, 2, NB])
        ga_bp = sb("ga_bp", [P, NB])

        xr = sb("xr", [P, NB * NT, D])
        vh = sb("vh", [P, NB, S])

        qm = sb("qm", [P, 2, 2, S], BF16)
        km = sb("km", [P, 2, 2, S], BF16)
        qe = sb("qe", [P, 2, 2, S], BF16)
        ke = sb("ke", [P, 2, 2, S], BF16)
        prob = sb("prob", [P, 20, S])
        v_ext = sb("v_ext", [P, NT, H, 32])
        stat = sb("stat", [P, NT, 6])
        mv = sb("mv", [P, NT, 2])
        var = sb("var", [P, NT])
        rstd = sb("rstd", [P, NT])
        xn = sb("xn", [P, NT, D])
        hT = sb("hT", [P, S])
        rot_a = sb("rot_a", [P, S])
        rot_b = sb("rot_b", [P, S])
        full = sb("full", [P, S])
        rest = sb("rest", [P, S])
        part = {"q": sb("q_part", [P, 3, S], BF16), "k": sb("k_part", [P, 3, S], BF16)}
        rmax = sb("rmax", [P, 2, 8, NT])
        rmax_rest = sb("rmax_rest", [P, 64])
        rmax_part = sb("rmax_part", [P, 3, 64], BF16)
        rmax_T = sb("rmax_T", [64, 3 * P], BF16)
        oT = sb("oT", [P, 2, S])
        rden = sb("rden", [P, NT, 4])
        onorm = sb("onorm", [P, NT, D])
        on_att = sb("on_att", [P, 2, S])
        onT, att = on_att[:, 0, :], on_att[:, 1, :]
        stat2 = sb("stat2", [P, NT, 6])
        mv2 = sb("mv2", [P, NT, 2])
        var2 = sb("var2", [P, NT])
        rstd2 = sb("rstd2", [P, NT])
        xn2 = sb("xn2", [P, NT, D])
        h2T = sb("h2T", [P, S])
        h2 = sb("h2", [P, NT, ROW])
        logit = sb("logit", [P, NT, NE])
        free_rows = [f[:, 0:GRP * ROW].rearrange("p (r c) -> p r c", c=ROW) for f in (
            logit[:, :, :].rearrange("p t k -> p (t k)"), h2[:, :, :].rearrange("p t c -> p (t c)"),
            on_att[:, :, :].rearrange("p a t -> p (a t)"))]
        logit_cut = on_att[:, :, :].rearrange("p a t -> p (a t)")[:, 0:NT * NE].rearrange("p (t k) -> p t k", k=NE)
        chosen = sb("chosen", [P, NT, NE], BF16)
        v8 = sb("v8", [P, NT, TOPK])
        i8 = sb("i8", [P, NT, TOPK], U32)
        pos8 = sb("pos8", [P, NT, TOPK])
        row_of = sb("row_of", [P, NT])
        sg = sb("sg", [P, NT, TOPK])
        sg_sum = sb("sg_sum", [P, NT])
        pos_s = sb("pos_s", [P, NT * TOPK], U32)
        step_p = sb("step_p", [P, 2, NE])
        place = xn2[:, :, :].rearrange("p t d -> p (t d)")[:, 0:2 * NE].rearrange("p (t k) -> p t k", k=NE)
        junk = on_att[:, :, :].rearrange("p a t -> p (a t)").bitcast(BF16)[:, 0:TOPK * NE] \
            .rearrange("p (k e) -> p k e", k=TOPK)
        page_bc = sb("page_bc", [P, 2, NE])
        rows = sb("rows", [1, 2, NE])
        filled = sb("filled", [1, NE], BF16)
        fill = sb("fill", [1, NE])
        total = sb("total", [1, NE])
        total_i = sb("total_i", [1, NE], I32)
        full_i = sb("full_i", [1, NE], I32)
        newp = sb("newp", [1, NE])
        endp = sb("endp", [1, NE])
        cur = sb("cur", [1, NE])
        curd = sb("curd", [1, NE])
        nextp = sb("nextp", [1, 1])

        bank = [ctx.enter_context(nc.psum_tensor(f"bank{i}", [P, 512], F32)) for i in range(8)]
        MX, ST, PV, MA, MB = bank[0:2], bank[2:5], bank[5], bank[6], bank[7]

        s_const, s_x, s_zero, s_set, s_zfill, s_rest = (
            sem(n) for n in ("s_const", "s_x", "s_zero", "s_set", "s_zfill", "s_rest"))
        s_modd, s_modp, s_moda = sem("s_modd"), sem("s_modp"), sem("s_moda")
        pre_d = Events(sem("pre_d"), ["stats", "aggr", "var", "xn", "q_a", "q_b", "q", "k_a", "k_b", "k", "v"])
        pre_g = Events(sem("pre_g"), ["rstd", "q_rest", "q_3", "k_rest", "k_3"])
        pre_a = Events(sem("pre_a"), ["hT", "q_1", "q_2", "k_1", "k_2"])
        pre_p = Events(sem("pre_p"), ["T", "q_a", "q_b", "k_a", "k_b", "v"])
        s_store = {"q": sem("s_store_q"), "k": sem("s_store_k")}
        s_mxp, s_mxd = sem("s_mxp"), sem("s_mxd")
        fin_d = Events(sem("fin_d"), ["m1", "rest", "m2", "m3"])
        s_finp, s_fina, s_mstore = sem("s_finp"), sem("s_fina"), sem("s_mstore")
        s_ldm = [sem(f"s_ldm{c}") for c in range(4)]
        s_lde = [sem(f"s_lde{c}") for c in range(4)]
        s_exp, s_exa = sem("s_exp"), sem("s_exa")
        s_pv, s_ov, s_ot, s_rd, s_on, s_vx = (sem(n) for n in ("s_pv", "s_ov", "s_ot", "s_rd", "s_on", "s_vx"))
        post_p = Events(sem("post_p"), ["onT", "proj", "attT", "h2T", "log0", "log1", "cnt", "bc", "z0", "z1", "h2"])
        post_a = Events(sem("post_a"), ["onT", "att", "h2T", "h2T_keep", "log0", "log1", "sig", "bc", "h2"])
        post_d = Events(sem("post_d"), ["x1", "stats", "aggr", "var", "xn", "v8", "i8", "cut", "chosen",
                                        "w1", "w2", "w3", "w4", "w5", "total", "total_i", "full_i", "newp", "endp",
                                        "curd0", "jump0", "jump", "openrow", "filled", "fill", "curd1", "curd2", "cur", "nextp",
                                        "step0", "zs0", "place0", "pos0", "step1", "zs1", "place1", "pos1",
                                        "pos_s", "base", "ids", "wts", "row_of"])
        post_g = Events(sem("post_g"), ["rstd"])
        s_scat = sem("s_scat")
        s_ends = sem("s_ends")
        s_tab, s_tabd, s_tabp = sem("s_tab"), sem("s_tabd"), sem("s_tabp")
        s_out = sem("s_out")

        SETDONE = 9 + 4 * FREE_SETS
        def plain_rows(e, first, last):
            for d, src in ((qd, zerob), (kd, oneb)):
                e.dma_start(d[first:last, :, MAXROW:64].rearrange("n a r (g t) -> (r g) (n a) t", t=S),
                            src[:, :].rearrange("p (o t) -> p o t", o=1)
                            .broadcast_to([P, 2 * (last - first), S])).then_inc(s_rest, 16)

        setup = [
            {"sp": lambda e: [
                e.dma_start(xr[:, 0:NT, :], x[0].rearrange("(t p) d -> p t d", p=P)).then_inc(s_x, 16),
                e.dma_start(w_all[:, :], wts).then_inc(s_const, 16),
                e.dma_start(c_all[:, :], const).then_inc(s_const, 16),
                e.dma_start(cb_all[:, :], constb).then_inc(s_const, 16),
                e.dma_start(bv_bc[:, :], bvec.partition_broadcast(P)).then_inc(s_const, 16),
                e.dma_start(eb_row[:, :], brow).then_inc(s_const, 16),
                e.dma_start(wds_sb[:, :], wds).then_inc(s_const, 16),
                e.wait_ge(s_set, 2),
                plain_rows(e, 0, 1),
                e.wait_ge(s_x, 16),
                e.dma_start(xr[:, NT:2 * NT, :], x[1].rearrange("(t p) d -> p t d", p=P)).then_inc(s_x, 16)]},
            {"pool": lambda e: [
                e.memset(v_ext[:, :, :, :], 0.0).then_inc(s_zero, 1),
                e.wait_ge(s_zero, 1),
                e.memset(v_ext[:, :, :, HD:HD + 1], 1.0).then_inc(s_zero, 1)],
             "dve": lambda e: [
                e.memset(zerob[:, :], 0.0).then_inc(s_set, 1),
                e.memset(oneb[:, :], 1.0).then_inc(s_set, 1),
                e.memset(mhalf[:, :], -0.5).then_inc(s_set, 1),
                e.memset(ones_row[:, :], 1.0).then_inc(s_set, 1),
                e.memset(zero_row[:, :], 0.0).then_inc(s_set, 1),
                e.memset(fill[:, :], 0.0).then_inc(s_set, 1),
                e.memset(nextp[:, :], float(NE)).then_inc(s_set, 1),
                e.wait_ge(s_const, 96),
                e.tensor_copy(cur[:, :], iota_e[0:1, :]).then_inc(s_set, 1),
                e.tensor_copy(row_of[:, :], row_0).then_inc(s_set, 1),
                [[e.memset(f[:, :, 0:BASE], 0.0).then_inc(s_set, 1),
                  e.memset(f[:, :, IDS:WTS], -1.0).then_inc(s_set, 1),
                  e.memset(f[:, :, WTS:ROW], 0.0).then_inc(s_set, 1),
                  e.tensor_scalar(f[:, :, BASE], row_free, float(i * GRP * P), None, ALU.add).then_inc(s_set, 1)]
                 for i, f in enumerate(free_rows)]]},
            {"act": lambda e: [e.wait_ge(s_const, 96),
                               e.activation(sig_c[:, :], col["cT"], ACT.Exp, scale=-1.0).then_inc(s_moda, 1)]},
            {"dve": lambda e: [e.wait_ge(s_moda, 1),
                               e.tensor_scalar(sig_c[:, :], sig_c[:, :], 1.0, None, ALU.add).then_inc(s_modd, 1),
                               e.wait_ge(s_modd, 1),
                               e.reciprocal(sig_c[:, :], sig_c[:, :]).then_inc(s_modd, 1),
                               e.wait_ge(s_modd, 2),
                               e.tensor_tensor(silu_c[:, :], sig_c[:, :], col["cT"], ALU.mult).then_inc(s_modd, 1)]},
            {"pe": lambda e: [e.wait_ge(s_modd, 3),
                              [e.matmul(MA[:, j * NB:(j + 1) * NB], col["wmod"][:, j * D:(j + 1) * D], silu_c[:, :],
                                        start=True, stop=True) for j in range(6)][-1].then_inc(s_modp, 1)]},
            {"dve": lambda e: [
                e.wait_ge(s_modp, 1),
                e.tensor_copy(mod[:, :, :], MA[:, 0:6 * NB].rearrange("p (j n) -> p j n", n=NB)).then_inc(s_modd, 1),
                e.wait_ge(s_modd, 4),
                e.tensor_scalar(gsign[:, :, :], mod[:, 2::3, :], 0.0, 2.0, ALU.is_ge, ALU.mult).then_inc(s_modd, 1),
                e.tensor_scalar(gneg[:, :, :], mod[:, 2::3, :], -1.0, 0.25, ALU.mult, ALU.max).then_inc(s_modd, 1),
                e.wait_ge(s_modd, 6),
                e.tensor_tensor(gabs[:, :, :], mod[:, 2::3, :], gneg[:, :, :], ALU.max).then_inc(s_modd, 1),
                e.wait_ge(s_modd, 7),
                e.scalar_tensor_tensor(out=mod[:, 2::3, :], in0=gsign[:, :, :], scalar=-1.0, in1=gabs[:, :, :],
                                       op0=ALU.add, op1=ALU.mult).then_inc(s_modd, 1),
                e.tensor_scalar(mod[:, 1::3, :], mod[:, 1::3, :], 1.0, None, ALU.add).then_inc(s_modd, 1),
                e.wait_ge(s_modd, 9),
                e.tensor_scalar(ga_bp[:, :], mod[:, 2, :], col["bp"], None, ALU.mult).then_inc(s_modd, 1)]},
        ]
        MODDONE = 10

        def xtile(n, t):
            return xr[:, bass.ds(n * NT + t, 1), :].rearrange("p o d -> p (o d)")

        def seq(n):
            return xr[:, bass.ds(n * NT, NT), :]

        def mcol(j, n):
            return mod[:, j, bass.ds(n, 1)]

        NZ = 24
        ZB = NPAGE // GRP // NZ

        def second_loads():
            def rest_of_x(e):
                e.dma_start(xr[:, 2 * NT:, :].rearrange("p (n t) d -> p n t d", t=NT),
                            x[2:NB].rearrange("n (t p) d -> p n t d", p=P)).then_inc(s_x, 16)
            return [{"sp": rest_of_x}] + [{"sp": lambda e, n=n: plain_rows(e, n, n + 3)} for n in range(1, NB, 3)]

        def clears():
            def clear(e, z):
                if z == 0:
                    e.wait_ge(s_set, SETDONE)
                first, which = z // FREE_SETS * ZB, z % FREE_SETS
                dst = pages[first * FREE_SETS * GRP * P:(first + ZB) * FREE_SETS * GRP * P, :] \
                    .rearrange("(b f p r) c -> f p b (r c)", b=ZB, f=FREE_SETS, p=P)[which]
                src = free_rows[which].rearrange("p (o r) c -> p o (r c)", o=1).broadcast_to([P, ZB, GRP * ROW])
                e.dma_start(dst, src).then_inc(s_zfill, 16)
            return [{"sp": lambda e, z=z: clear(e, z)} for z in range(NZ)]

        def pre(n):
            steps = []

            def ln(e):
                if isinstance(n, int):
                    e.wait_ge(s_x, 16 * min(n + 1, 3))
                pre_d.wait(e, "v", n - 1)
                apart(e)
                for t in range(NT):
                    last = e.bn_stats(stat[:, t, :], xtile(n, t))
                pre_d.done(last, "stats")
                pre_d.wait(e, "stats", n)
                apart(e)
                for t in range(NT):
                    last = e.bn_aggr(mv[:, t, :], stat[:, t, :])
                pre_d.done(last, "aggr")
                pre_d.wait(e, "aggr", n)
                pre_d.done(e.tensor_scalar(var[:, :], mv[:, :, 1], EPS, None, ALU.add), "var")

            def rs(e):
                pre_d.wait(e, "var", n)
                if isinstance(n, int) and n == 0:
                    e.wait_ge(s_set, 3)
                pre_g.done(e.tensor_tensor(rstd[:, :], var[:, :], mhalf[:, :], ALU.pow), "rstd")
            steps.append({"dve": ln, "pool": rs})

            def norm(e):
                pre_g.wait(e, "rstd", n)
                pre_p.wait(e, "T", n - 1)
                for t in range(NT):
                    last = e.tensor_scalar(xn[:, t, :], xtile(n, t), mv[:, t, 0:1], rstd[:, t:t + 1],
                                           ALU.subtract, ALU.mult)
                pre_d.done(last, "xn")

            def tr(e):
                pre_d.wait(e, "xn", n)
                if isinstance(n, int) and n == 0:
                    e.wait_ge(s_const, 96)
                    e.wait_ge(s_modd, MODDONE)
                for t in range(NT):
                    last = e.transpose(MA[:, t * P:(t + 1) * P], xn[:, t, :], ident)
                pre_p.done(last, "T")

            def modulate(e):
                pre_p.wait(e, "T", n)
                pre_a.done(e.activation(hT[:, :], MA[:, :], ACT.Identity, bias=mcol(0, n), scale=mcol(1, n)), "hT")
            steps.append({"dve": norm, "pe": tr, "act": modulate})

            stores = []
            for w, prev in (("q", None), ("k", "q")):
                def proj_a(e, w=w, prev=prev):
                    if prev is None:
                        pre_a.wait(e, "hT", n)
                    else:
                        pre_d.wait(e, prev + "_b", n)
                    pre_p.done(e.matmul(MA[:, :], col["w" + w], hT[:, :], start=True, stop=True), w + "_a")

                def rope_a(e, w=w):
                    pre_p.wait(e, w + "_a", n)
                    if w == "k":
                        pre_d.wait(e, "q", n)
                    pre_d.done(e.scalar_tensor_tensor(out=rot_a[:, :], in0=MA[:, :], scalar=col["b" + w], in1=cosT,
                                                      op0=ALU.add, op1=ALU.mult), w + "_a")

                def proj_b(e, w=w):
                    pre_d.wait(e, w + "_a", n)
                    pre_p.done(e.matmul(MA[:, :], col["w" + w + "r"], hT[:, :], start=True, stop=True), w + "_b")

                def rope_b(e, w=w):
                    pre_p.wait(e, w + "_b", n)
                    pre_d.done(e.scalar_tensor_tensor(out=rot_b[:, :], in0=MA[:, :], scalar=col["b" + w + "r"],
                                                      in1=sinT, op0=ALU.add, op1=ALU.mult), w + "_b")

                def turned(e, w=w):
                    pre_d.wait(e, w + "_b", n)
                    pre_g.wait(e, "k_rest" if w == "q" else "q_rest", n - 1 if w == "q" else n)
                    pre_d.done(e.tensor_tensor(full[:, :], rot_a[:, :], rot_b[:, :], ALU.add), w)

                def part1(e, w=w):
                    pre_d.wait(e, w, n)
                    wait(e, s_store[w], 16 * 6 * n)
                    pre_a.done(e.activation(part[w][:, 0, :], full[:, :], ACT.Identity), w + "_1")

                def rest1(e, w=w):
                    pre_a.wait(e, w + "_1", n)
                    pre_g.wait(e, "k_3" if w == "q" else "q_3", n - 1 if w == "q" else n)
                    pre_g.done(e.tensor_tensor(rest[:, :], full[:, :], part[w][:, 0, :], ALU.subtract),
                               w + "_rest")

                def part2(e, w=w):
                    pre_g.wait(e, w + "_rest", n)
                    pre_a.done(e.activation(part[w][:, 1, :], rest[:, :], ACT.Identity), w + "_2")

                def part3(e, w=w):
                    pre_a.wait(e, w + "_2", n)
                    pre_g.done(e.tensor_tensor(part[w][:, 2, :], rest[:, :], part[w][:, 1, :], ALU.subtract),
                               w + "_3")

                def store(e, w=w):
                    pre_g.wait(e, w + "_3", n)
                    stacks = (qd if w == "q" else kd)[bass.ds(n, 1)].rearrange("o a r (g t) -> (o a) r g t", t=S)
                    for first, parts in (Q_RUNS if w == "q" else K_RUNS):
                        m = len(parts)
                        for par in range(2):
                            dst = stacks[par, first * 8:(first + m) * 8].rearrange("(s r) g t -> (r g) s t", s=m)
                            src = part[w][par * 64:(par + 1) * 64, parts[0]:parts[0] + (1 if w == "q" else m), :]
                            e.dma_start(dst, src.broadcast_to([64, m, S]) if w == "q" and m > 1 else src) \
                             .then_inc(s_store[w], 16)
                steps.append({"pe": proj_a, "dve": rope_a})
                steps.append({"pe": proj_b, "dve": rope_b})
                steps.append({"dve": turned, "act": part1, "pool": rest1})
                steps.append({"act": part2, "pool": part3})
                stores.append({"sp": store})

            def v_proj(e):
                pre_d.wait(e, "k_b", n)
                for t in range(NT):
                    last = e.matmul(MA[:, t * P:(t + 1) * P], hT[:, t * P:(t + 1) * P], col["wv"],
                                    start=True, stop=True)
                pre_p.done(last, "v")

            def v_keep(e):
                pre_p.wait(e, "v", n)
                pre_d.done(e.tensor_tensor(
                    vh[:, bass.ds(n, 1), :].rearrange("p o (t d) -> p (o t) d", d=D),
                    MA[:, :].rearrange("p (t d) -> p t d", d=D),
                    bv_bc[:, :].rearrange("p (o d) -> p o d", o=1).broadcast_to([P, NT, D]), ALU.add), "v")
            steps.insert(len(steps) - 1, {"pe": v_proj, "dve": v_keep})
            steps = steps[:7] + stores[0:1] + steps[7:] + stores[1:2]
            return steps

        def max_units(c):
            heads = [(h, par) for par in range(2) for h in range(2)]
            units = [(3, [hp]) for hp in heads] + [(2, [hp]) for hp in heads]
            units += [(1, [(0, par), (1, par)]) for par in range(2)]
            return units + [(0, [(0, par), (1, par)]) for par in range(2)]

        NU = 12

        def max_loads(n, quads):
            def load(e, c):
                if isinstance(n, int) and n < 2 and c == 0:
                    e.wait_ge(s_rest, 32 if n == 0 else 192)
                for w in "qk":
                    wait(e, s_store[w], 16 * 6 * (n + 1))
                wait(e, s_mxp, n * 4 * NU + (c - 1) * NU)
                e.dma_start(qm[:, c % 2, :, :].rearrange("p h t -> p (h t)"), stack(qd, n, c)).then_inc(s_ldm[c], 16)
                e.dma_start(km[:, c % 2, :, :].rearrange("p h t -> p (h t)"), stack(kd, n, c)).then_inc(s_ldm[c], 16)
            return [{"sp": lambda e, c=c: load(e, c)} for c in quads]

        def mx(n):
            steps = []
            for c in range(4):
                for u, (i, heads) in enumerate(max_units(c)):
                    g = c * NU + u
                    width = (i + 1) * P

                    def scores(e, c=c, u=u, i=i, heads=heads, g=g, width=width):
                        if u == 0:
                            e.wait_ge(s_ldm[c], 32 * (n + 1))
                        if g < 2:
                            wait(e, s_fina, n)
                        else:
                            wait(e, s_mxd, n * 4 * NU + g - 1)
                        for k, (h, par) in enumerate(heads):
                            rows_ = slice(64 * par, 64 * par + 64)
                            e.matmul(MX[g % 2][:, k * width:(k + 1) * width],
                                     qm[rows_, c % 2, h, i * P:(i + 1) * P], km[rows_, c % 2, h, 0:width],
                                     start=True, stop=True)
                            last = e.matmul(MX[g % 2][:, (k + 1) * width - P:(k + 1) * width], identb, mask_q,
                                            start=False, stop=True, skip_group_check=True)
                        last.then_inc(s_mxp, 1)

                    def reduce(e, c=c, i=i, heads=heads, g=g, width=width):
                        e.wait_ge(s_mxp, n * 4 * NU + g + 1)
                        if g == 0:
                            fin_d.wait(e, "rest", n - 1)
                        h, par = heads[0]
                        e.tensor_reduce(rmax[:, par, 2 * c + h:2 * c + h + len(heads), i],
                                        MX[g % 2][:, 0:len(heads) * width].rearrange("p (k w) -> p k w", w=width),
                                        AX.X, ALU.max).then_inc(s_mxd, 1)
                    steps.append({"pe": scores, "dve": reduce})
                    if u == 1 and c in (1, 2):
                        steps += max_loads(n, [c + 1])

            def split(e):
                flat = rmax[:, :, :, :].rearrange("p a h i -> p (a h i)")
                e.wait_ge(s_mxd, (n + 1) * 4 * NU)
                wait(e, s_finp, n)
                fin_d.done(e.tensor_scalar(rmax_part[:, 0, :], flat, -1.0, None, ALU.mult), "m1")
                fin_d.wait(e, "m1", n)
                fin_d.done(e.scalar_tensor_tensor(out=rmax_rest[:, :], in0=flat, scalar=-1.0,
                                                  in1=rmax_part[:, 0, :], op0=ALU.mult, op1=ALU.subtract), "rest")
                fin_d.wait(e, "rest", n)
                fin_d.done(e.tensor_copy(rmax_part[:, 1, :], rmax_rest[:, :]), "m2")
                fin_d.wait(e, "m2", n)
                fin_d.done(e.tensor_tensor(rmax_part[:, 2, :], rmax_rest[:, :], rmax_part[:, 1, :],
                                           ALU.subtract), "m3")

            mx_b = MX[0][:, :].bitcast(BF16)

            def turn(e):
                fin_d.wait(e, "m3", n)
                apart(e)
                for j in range(3):
                    last = e.transpose(mx_b[0:64, j * P:(j + 1) * P], rmax_part[:, j, :], identb)
                last.then_inc(s_finp, 1)

            def keep(e):
                e.wait_ge(s_finp, n + 1)
                wait(e, s_mstore, 32 * n)
                e.activation(rmax_T[:, :], mx_b[0:64, 0:3 * P], ACT.Identity).then_inc(s_fina, 1)

            def store(e):
                wait(e, s_fina, n + 1)
                for par in range(2):
                    dst = qd[bass.ds(n, 1), par].rearrange("o r t -> (o r) t")[MAXROW:MAXROW + 3, :]
                    e.dma_start(dst.rearrange("r (g t) -> g r t", t=P),
                                rmax_T[32 * par:32 * par + 32, :].rearrange("g (r t) -> g r t", t=P)) \
                     .then_inc(s_mstore, 16)
            steps.append({"dve": split, "pe": turn, "act": keep, "sp": store})
            return steps

        def stack(d, n, c):
            return d[bass.ds(n, 1)].rearrange("o a r t -> (o a r) t")[:, 2 * c * S:(2 * c + 2) * S]

        EU = 10
        def exp_place(h, par, j):
            if j == 0:
                return 4 * par + 2 * h, 0
            if j == 1:
                return 4 * par + 2 * h + 1, 0
            if j == 3:
                return 4 * par + 2 * h + 1, 3 * P
            return 8 + par, 2 * P * h

        def exp_loads(n, quads):
            def load(e, c):
                wait(e, s_mstore, 32 * (n + 1))
                wait(e, s_exp, n * 4 * EU + (c - 1) * EU)
                e.dma_start(qe[:, c % 2, :, :].rearrange("p h t -> p (h t)"), stack(qd, n, c)).then_inc(s_lde[c], 16)
                e.dma_start(ke[:, c % 2, :, :].rearrange("p h t -> p (h t)"), stack(kd, n, c)).then_inc(s_lde[c], 16)
            return [{"sp": lambda e, c=c: load(e, c)} for c in quads]

        def ex(n):
            steps = []

            def prev_user(g):
                if g >= 3:
                    return 3
                return g + 4 * EU - max(k for k in range(4 * EU) if k % 3 == g % 3)

            def pv(c):
                def vx(e):
                    wait(e, s_pv, 4 * (n - 1) + c + 1)
                    if isinstance(n, int) and n == 0:
                        e.wait_ge(s_zero, 2)
                    pre_d.wait(e, "v", n)
                    e.tensor_copy(v_ext[:, :, 4 * c:4 * c + 4, 0:HD],
                                  vh[:, bass.ds(n, 1), :].rearrange("p o (t h d) -> p (o t) h d", t=NT, d=HD)
                                  [:, :, 4 * c:4 * c + 4, :]).then_inc(s_vx, 1)

                def product(e, j):
                    if j == 0:
                        e.wait_ge(s_exa, n * 4 * EU + (c + 1) * EU)
                        e.wait_ge(s_vx, 4 * n + c + 1)
                        wait(e, s_on, 4 * n + c)
                    for g in range(4):
                        u, c0 = exp_place(g // 2, g % 2, j)
                        last = e.matmul(PV[32 * g:32 * g + 32, j * P:S], v_ext[:, j, 4 * c + g, :],
                                        prob[:, (c % 2) * EU + u, c0:c0 + S - j * P],
                                        start=(j == 0), stop=(j == NT - 1), skip_group_check=True)
                    if j == NT - 1:
                        last.then_inc(s_pv, 1)

                def take(e):
                    e.wait_ge(s_pv, 4 * n + c + 1)
                    wait(e, s_ot, 4 * n + c - 1)
                    e.activation(oT[:, c % 2, :], PV[:, :], ACT.Identity).then_inc(s_ov, 1)

                def turn(e):
                    e.wait_ge(s_ov, 4 * n + c + 1)
                    for t in range(NT):
                        last = e.transpose(PV[:, t * P:(t + 1) * P], oT[:, c % 2, t * P:(t + 1) * P], ident)
                    last.then_inc(s_ot, 1)

                def norm(e):
                    heads = PV[:, :].rearrange("p (t g d) -> p t g d", t=NT, g=4)
                    e.wait_ge(s_ot, 4 * n + c + 1)
                    wait(e, s_on, 4 * n + c)
                    e.reciprocal(rden[:, :, :], heads[:, :, :, HD]).then_inc(s_rd, 1)
                    e.wait_ge(s_rd, 4 * n + c + 1)
                    if c == 0:
                        post_p.wait(e, "onT", n - 1)
                    e.tensor_tensor(onorm[:, :, 32 * c:32 * c + 32].rearrange("p t (g d) -> p t g d", g=4),
                                    heads[:, :, :, 0:HD],
                                    rden[:, :, :].rearrange("p t (g o) -> p t g o", o=1)
                                    .broadcast_to([P, NT, 4, HD]), ALU.mult).then_inc(s_on, 1)
                return [{"pool": vx}] + [{"pe": lambda e, j=j: product(e, j)} for j in range(NT)] \
                    + [{"act": take}, {"pe": turn, "dve": norm}]

            todo = []
            for c in range(4):
                units = {}
                for par in range(2):
                    for h in range(2):
                        for j in range(NT):
                            u, c0 = exp_place(h, par, j)
                            units.setdefault(u, []).append((h, par, j, c0))
                for u in range(EU):
                    g = c * EU + u

                    def scores(e, c=c, u=u, g=g, pieces=units[u]):
                        if u == 0:
                            e.wait_ge(s_lde[c], 32 * (n + 1))
                        wait(e, s_exa, n * 4 * EU + g - prev_user(g) + 1)
                        for (h, par, j, c0) in pieces:
                            rows_ = slice(64 * par, 64 * par + 64)
                            e.matmul(ST[g % 3][:, c0:c0 + S - j * P], ke[rows_, c % 2, h, j * P:(j + 1) * P],
                                     qe[rows_, c % 2, h, j * P:S], start=True, stop=True)
                            last = e.matmul(ST[g % 3][:, c0:c0 + P], identb, mask_k, start=False, stop=True,
                                            skip_group_check=True)
                        last.then_inc(s_exp, 1)

                    def expo(e, c=c, u=u, g=g):
                        e.wait_ge(s_exp, n * 4 * EU + g + 1)
                        if u == 0:
                            wait(e, s_pv, 4 * n + c - 1)
                        e.activation(prob[:, (c % 2) * EU + u, :], ST[g % 3][:, :], ACT.Exp, scale=SCALE) \
                         .then_inc(s_exa, 1)
                    steps.append({"pe": scores, "act": expo})
                    if c > 0 and u >= 1 and todo:
                        steps.append(todo.pop(0))
                todo += pv(c)
            return steps + todo

        def scatter(e, n, t, k):
            if t == 0 and k == 0:
                post_d.wait(e, "wts", n)
                post_a.wait(e, "h2", n)
                if isinstance(n, int) and n == 0:
                    e.wait_ge(s_zfill, 16 * NZ)
                apart(e)
            e.indirect_dma_start(
                out=pages, in_=h2[:, t, :], in_offset=None,
                out_offset=bass.IndirectOffsetOnAxis(ap=pos_s[:, t * TOPK + k:t * TOPK + k + 1], axis=0),
            ).then_inc(s_scat, 16)

        def post(n):
            steps = []
            P_, A_, D_, G_ = post_p, post_a, post_d, post_g

            def on_turn(e):
                e.wait_ge(s_on, 4 * (n + 1))
                A_.wait(e, "h2", n - 1)
                for t in range(NT):
                    last = e.transpose(MB[:, t * P:(t + 1) * P], onorm[:, t, :], ident)
                P_.done(last, "onT")

            def on_keep(e):
                P_.wait(e, "onT", n)
                D_.wait(e, "pos1", n - 1)
                if isinstance(n, int) and n == 0:
                    e.wait_ge(s_zfill, 16 * NZ)
                A_.done(e.activation(onT, MB[:, :], ACT.Identity), "onT")
            steps.append({"pe": on_turn, "act": on_keep})

            def proj(e):
                A_.wait(e, "onT", n)
                P_.done(e.matmul(MB[:, :], col["wp"], onT, start=True, stop=True), "proj")

            def gate(e):
                P_.wait(e, "proj", n)
                A_.done(e.activation(att, MB[:, :], ACT.Identity, bias=ga_bp[:, bass.ds(n, 1)],
                                     scale=mcol(2, n)), "att")
            steps.append({"pe": proj, "act": gate})

            def att_turn(e):
                A_.wait(e, "att", n)
                for t in range(NT):
                    last = e.transpose(MB[:, t * P:(t + 1) * P], att[:, t * P:(t + 1) * P], ident)
                P_.done(last, "attT")

            def residual(e):
                P_.wait(e, "attT", n)
                D_.done(e.tensor_tensor(seq(n), seq(n), MB[:, :].rearrange("p (t d) -> p t d", d=D), ALU.add), "x1")

            def measure(e):
                D_.wait(e, "x1", n)
                apart(e)
                for t in range(NT):
                    last = e.bn_stats(stat2[:, t, :], xtile(n, t))
                D_.done(last, "stats")
                D_.wait(e, "stats", n)
                apart(e)
                for t in range(NT):
                    last = e.bn_aggr(mv2[:, t, :], stat2[:, t, :])
                D_.done(last, "aggr")
                D_.wait(e, "aggr", n)
                D_.done(e.tensor_scalar(var2[:, :], mv2[:, :, 1], EPS, None, ALU.add), "var")

            def rs(e):
                D_.wait(e, "var", n)
                G_.done(e.tensor_tensor(rstd2[:, :], var2[:, :], mhalf[:, :], ALU.pow), "rstd")
            steps += [{"pe": att_turn, "dve": residual}, {"dve": measure, "pool": rs}]

            def norm(e):
                G_.wait(e, "rstd", n)
                for t in range(NT):
                    last = e.tensor_scalar(xn2[:, t, :], xtile(n, t), mv2[:, t, 0:1], rstd2[:, t:t + 1],
                                           ALU.subtract, ALU.mult)
                D_.done(last, "xn")

            def turn(e):
                D_.wait(e, "xn", n)
                for t in range(NT):
                    last = e.transpose(MB[:, t * P:(t + 1) * P], xn2[:, t, :], ident)
                P_.done(last, "h2T")

            def modulate(e):
                P_.wait(e, "h2T", n)
                A_.done(e.activation(h2T[:, :], MB[:, :], ACT.Identity, bias=mcol(3, n), scale=mcol(4, n)), "h2T")
                wait(e, s_vx, 4 * (n + 1))
                A_.done(e.activation(vh[:, bass.ds(n, 1), :].rearrange("p o t -> p (o t)"), MB[:, :],
                                     ACT.Identity, bias=mcol(3, n), scale=mcol(4, n)), "h2T_keep")
            steps.append({"dve": norm, "pe": turn, "act": modulate})

            for half in range(2):
                def route(e, half=half):
                    A_.wait(e, "h2T_keep" if half == 0 else "log0", n)
                    for k in range(2):
                        t = 2 * half + k
                        e.matmul(MB[:, k * NE:(k + 1) * NE], ones_row[:, :], eb_row[:, :], start=True, stop=False)
                        last = e.matmul(MB[:, k * NE:(k + 1) * NE], h2T[:, t * P:(t + 1) * P], col["rw"],
                                        start=False, stop=True)
                    P_.done(last, f"log{half}")

                def route_keep(e, half=half):
                    P_.wait(e, f"log{half}", n)
                    if half == 0:
                        D_.wait(e, "cut", n - 1)
                    A_.done(e.activation(logit[:, 2 * half:2 * half + 2, :],
                                         MB[:, 0:2 * NE].rearrange("p (t k) -> p t k", k=NE), ACT.Identity),
                            f"log{half}")
                steps.append({"pe": route, "act": route_keep})

            def top(e):
                A_.wait(e, "log1", n)
                apart(e)
                for t in range(NT):
                    last = e.max(v8[:, t, :], logit[:, t, :])
                D_.done(last, "v8")

            def top_at(e):
                D_.wait(e, "v8", n)
                apart(e)
                for t in range(NT):
                    last = e.max_index(i8[:, t, :], v8[:, t, :], logit[:, t, :])
                D_.done(last, "i8")

            def cut(e):
                for t in range(NT):
                    last = e.match_replace(logit_cut[:, t, :], v8[:, t, :], logit[:, t, :], NEG)
                D_.done(last, "cut")

            def choose(e):
                D_.wait(e, "cut", n)
                P_.wait(e, "z1", n - 1)
                D_.done(e.tensor_scalar(chosen[:, :, :], logit_cut[:, :, :], NEG, None, ALU.is_equal), "chosen")

            def count(e):
                D_.wait(e, "chosen", n)
                for t in range(NT):
                    last = e.matmul(MB[0:1, 0:NE], onesb[:, 0:1], chosen[:, t, :], start=(t == 0), stop=(t == NT - 1))
                P_.done(last, "cnt")
            steps += [{"dve": top}, {"dve": top_at}, {"dve": cut}, {"dve": choose, "pe": count}]

            def sig(e):
                D_.wait(e, "v8", n)
                D_.wait(e, "wts", n - 1)
                A_.done(e.activation(sg[:, :, :], v8[:, :, :], ACT.Exp, scale=-1.0), "sig")

            def weigh(e):
                A_.wait(e, "sig", n)
                D_.done(e.tensor_scalar(sg[:, :, :], sg[:, :, :], 1.0, None, ALU.add), "w1")
                D_.wait(e, "w1", n)
                D_.done(e.reciprocal(sg[:, :, :], sg[:, :, :]), "w2")
                D_.wait(e, "w2", n)
                D_.done(e.tensor_reduce(sg_sum[:, :], sg[:, :, :], AX.X, ALU.add), "w3")
                D_.wait(e, "w3", n)
                D_.done(e.tensor_scalar(sg_sum[:, :], sg_sum[:, :], 1e-9, None, ALU.add), "w4")
                D_.wait(e, "w4", n)
                D_.done(e.reciprocal(sg_sum[:, :], sg_sum[:, :]), "w5")
            steps.append({"act": sig, "dve": weigh})

            paging = (
                ("total", lambda e: e.tensor_tensor(total[:, :], fill[:, :], MB[0:1, 0:NE], ALU.add)),
                ("total_i", lambda e: e.tensor_scalar(total_i[:, :], total[:, :], float(P - 1), None, ALU.add)),
                ("full_i", lambda e: e.tensor_scalar(full_i[:, :], total_i[:, :], 7, None, ALU.logical_shift_right)),
                ("newp", lambda e: e.tensor_scalar(newp[:, :], full_i[:, :], -1.0, 0.0, ALU.add, ALU.max)),
                ("endp", lambda e: e.tensor_tensor_scan(endp[:, :], newp[:, :], zero_row[:, :], nextp[:, :],
                                                        ALU.add, ALU.add)),
                ("curd0", lambda e: e.tensor_tensor(curd[:, :], endp[:, :], newp[:, :], ALU.subtract)),
                ("jump0", lambda e: e.tensor_tensor(rows[:, 0, :], curd[:, :], cur[:, :], ALU.subtract)),
                ("jump", lambda e: e.tensor_scalar(rows[:, 0, :], rows[:, 0, :], float(P), -float(P), ALU.mult, ALU.add)),
                ("openrow", lambda e: e.tensor_scalar(rows[:, 1, :], cur[:, :], float(P), float(P), ALU.mult, ALU.add)),
                ("filled", lambda e: e.tensor_scalar(filled[:, :], fill[:, :], -float(P), None, ALU.add)),
                ("fill", lambda e: e.scalar_tensor_tensor(out=fill[:, :], in0=newp[:, :], scalar=-float(P),
                                                          in1=total[:, :], op0=ALU.mult, op1=ALU.add)),
                ("curd1", lambda e: e.scalar_tensor_tensor(out=curd[:, :], in0=endp[:, :], scalar=-1.0, in1=cur[:, :],
                                                           op0=ALU.add, op1=ALU.subtract)),
                ("curd2", lambda e: e.scalar_tensor_tensor(out=curd[:, :], in0=newp[:, :], scalar=0.0, in1=curd[:, :],
                                                           op0=ALU.is_gt, op1=ALU.mult)),
                ("cur", lambda e: e.tensor_tensor(cur[:, :], cur[:, :], curd[:, :], ALU.add)),
                ("nextp", lambda e: e.tensor_copy(nextp[:, :], endp[:, NE - 1:NE])))

            def page_op(e, k):
                name, f = paging[k]
                if k == 0:
                    P_.wait(e, "cnt", n)
                elif name not in ("openrow", "filled"):
                    D_.wait(e, paging[k - 1][0], n)
                if name == "endp":
                    wait(e, s_ends, 16 * n)
                if name == "jump0":
                    P_.wait(e, "z1", n - 1)
                D_.done(f(e), name)

            def spread(e):
                D_.wait(e, "filled", n)
                P_.done(e.matmul(MB[:, 0:2 * NE], ones_row[:, :], rows[:, 0:2, :].rearrange("p a k -> p (a k)"),
                                 start=True, stop=True), "bc")

            def spread_keep(e):
                P_.wait(e, "bc", n)
                D_.wait(e, "place1", n - 1)
                A_.done(e.activation(page_bc[:, :, :].rearrange("p a k -> p (a k)"), MB[:, 0:2 * NE],
                                     ACT.Identity), "bc")
            def ends_store(e):
                D_.wait(e, "endp", n)
                e.dma_start(ends_d[:, bass.ds(n * NE, NE)], endp[:, :]).then_inc(s_ends, 16)
            for k in range(0, len(paging), 3):
                steps.append({"dve": lambda e, k=k: [page_op(e, kk) for kk in range(k, min(k + 3, len(paging)))]})
            steps.append({"pe": spread, "act": spread_keep, "sp": ends_store})

            for half in range(2):
                def rank(e, half=half):
                    if half == 0:
                        A_.wait(e, "bc", n)
                    else:
                        D_.wait(e, "zs0", n)
                    for k in range(2):
                        dst = MB[:, k * NE:(k + 1) * NE]
                        e.matmul(dst, onesb[0:1, :], filled[:, :], start=True, stop=False)
                        for t in range(2 * half + k):
                            e.matmul(dst, onesb, chosen[:, t, :], start=False, stop=False)
                        last = e.matmul(dst, upper, chosen[:, 2 * half + k, :], start=False, stop=True)
                    P_.done(last, f"z{half}")

                def where(e, half=half):
                    z = MB[:, 0:2 * NE].rearrange("p (t k) -> p t k", k=NE)
                    wide = [page_bc[:, a:a + 1, :].broadcast_to([P, 2, NE]) for a in range(2)]
                    P_.wait(e, f"z{half}", n)
                    A_.wait(e, "bc", n)
                    D_.done(e.scalar_tensor_tensor(out=step_p[:, :, :], in0=z, scalar=TAKEN, in1=wide[0],
                                                   op0=ALU.is_ge, op1=ALU.mult), f"step{half}")
                    if half == 1:
                        D_.wait(e, "pos0", n)
                    D_.done(e.tensor_tensor(place[:, :, :], z, wide[1], ALU.add), f"zs{half}")
                    D_.wait(e, f"zs{half}", n)
                    D_.done(e.tensor_tensor(place[:, :, :], place[:, :, :], step_p[:, :, :], ALU.add), f"place{half}")

                def pick(e, half=half):
                    D_.wait(e, f"place{half}", n)
                    apart(e)
                    for k in range(2):
                        last = e.max(pos8[:, 2 * half + k, :], place[:, k, :])
                    D_.done(last, f"pos{half}")
                steps.append({"pe": rank, "dve": where})
                steps.append({"dve": pick})

            def back(e):
                D_.wait(e, "zs1", n)
                for t in range(NT):
                    last = e.transpose(MB[:, t * P:(t + 1) * P], h2T[:, t * P:(t + 1) * P], ident)
                P_.done(last, "h2")

            def back_keep(e):
                P_.wait(e, "h2", n)
                wait(e, s_scat, 16 * NT * TOPK * n)
                A_.done(e.activation(h2[:, :, 0:D], MB[:, :].rearrange("p (t d) -> p t d", d=D), ACT.Identity), "h2")
            steps.append({"pe": back, "act": back_keep})

            def keep(e):
                D_.wait(e, "pos1", n)
                wait(e, s_scat, 16 * NT * TOPK * n)
                D_.done(e.tensor_scalar(pos_s[:, :], pos8[:, :, :].rearrange("p t k -> p (t k)"), -TAKEN, None, ALU.add), "pos_s")
                D_.done(e.tensor_copy(h2[:, :, BASE], row_of[:, :]), "base")
                D_.done(e.tensor_scalar(h2[:, :, IDS:WTS], i8[:, :, :], float(P), None, ALU.mult), "ids")
                D_.done(e.scalar_tensor_tensor(
                    out=h2[:, :, WTS:ROW], in0=sg[:, :, :], scalar=2.5,
                    in1=sg_sum[:, :].rearrange("p (t o) -> p t o", o=1).broadcast_to([P, NT, TOPK]),
                    op0=ALU.mult, op1=ALU.mult), "wts")
                D_.wait(e, "base", n)
                D_.done(e.tensor_scalar(row_of[:, :], row_of[:, :], float(S * TOPK), None, ALU.add), "row_of")

            steps.append({"dve": keep})
            return steps

        def scatters(n):
            return [{"pool": lambda e, t=t, k=k: scatter(e, n, t, k)} for t in range(NT) for k in range(TOPK)]

        def turn_a(i, ex_=True, pre_=True, mx_=True, post_=True, scat_=True):
            streams = []
            if ex_:
                streams.append((ex(i), 0.0, 0.97, 0.95))
                streams.append((exp_loads(i, (2,)), 0.27, 0.27))
                streams.append((exp_loads(i, (3,)), 0.52, 0.52))
            if mx_:
                streams.append((mx(i + 1), 0.02, 0.86, 0.95))
                streams.append((exp_loads(i + 1, (0,)), 0.9, 0.9))
                streams.append((exp_loads(i + 1, (1,)), 0.975, 0.975))
            if isinstance(i, int) and i <= 0:
                first = (0, 1, 11, NZ)
                streams.append((clears()[first[i + 2]:first[i + 3]], 0.1, 0.9))
                if i == -1:
                    streams.append((second_loads(), 0.05, 0.6))
            if pre_:
                streams.append((pre(i + 2), 0.0, 0.85))
                streams.append((max_loads(i + 2, (0, 1)), 0.93, 0.96))
            if post_:
                streams.append((post(i - 1), 0.0, 0.97))
            if scat_:
                streams.append((scatters(i - 2), 0.0, 0.8))
            return merge(*streams)

        small = sb("small", [P, 4, PCOL])
        tab = qm[0:1, :, :, :].rearrange("p a h t -> p (a h t)").bitcast(I32)[:, 0:PCOL * P]
        page_expert = km[:, :, :, :].rearrange("p a h t -> p (a h t)").bitcast(F32)[:, 0:NPAGE]
        table_i = sb("table_i", [P, PCOL], I32)
        arena = prob[:, :, :].rearrange("p a b -> p (a b)")
        ends_bc = arena[:, 0:NB * NE]
        ends_junk = arena[:, NB * NE:4 * NB * NE].bitcast(BF16).rearrange("p (c e) -> p c e", c=PCOL)
        w_in = arena[:, 0:4 * GRP * WROW].rearrange("p (g j w) -> p g j w", g=4, j=GRP)
        o_ = 2 * NB * NE
        x_T = [arena[:, o_ + i * 512:o_ + (i + 1) * 512] for i in range(2)]
        h_g = [arena[:, o_ + 1024 + i * 256:o_ + 1024 + (i + 1) * 256] for i in range(2)]
        x_in = arena[:, o_ + 1536:o_ + 1536 + 4 * GRP * ROW].rearrange("p (g j c) -> p g j c", g=4, j=GRP)
        y_sb = v_ext[:, :, :, :].rearrange("p t h d -> p (t h d)").rearrange("p (g j d) -> p g j d", g=4, j=GRP)
        hit, hit_k, hit_w = (sb(n, [P, GRP, TOPK]) for n in ("hit", "hit_k", "hit_w"))
        rank_of = sb("rank_of", [P, GRP])
        w_of = sb("w_of", [P, 4, GRP])
        res_row = sb("res_row", [P, 4, GRP], U32)
        s_xl = [sem(f"s_xl{g}") for g in range(4)]
        s_ys = [sem(f"s_ys{g}") for g in range(4)]
        s_T, s_XT, s_G, s_H, s_Y, s_YD, s_YA = (sem(n) for n in ("s_T", "s_XT", "s_G", "s_H", "s_Y", "s_YD", "s_YA"))
        own_d = Events(sem("own_d"), ["hit", "hit_k", "hit_w", "rank", "w", "row"])

        LAST = NB - 1
        table = [
            {"sp": lambda e: [
                e.wait_ge(s_ends, 16 * NB),
                wait(e, s_pv, 4 * NB),
                e.dma_start(ends_bc, ends_d[0, :].partition_broadcast(P)).then_inc(s_tab, 16)]},
            {"dve": lambda e: [
                e.wait_ge(s_tab, 16),
                post_d.wait(e, "row_of", LAST),
                [e.tensor_scalar(ends_junk[:, c, :], ends_bc, page_no[:, c:c + 1], 0.0, ALU.is_le, ALU.add,
                                 accum_out=small[:, 0, c:c + 1]) for c in range(PCOL)],
                [e.tensor_scalar(junk[:, c, 0:NB], ends_bc.rearrange("p (n k) -> p n k", k=NE)[:, :, NE - 1],
                                 page_no[:, c:c + 1], 0.0, ALU.is_le, ALU.add,
                                 accum_out=small[:, 1, c:c + 1]) for c in range(PCOL)][-1].then_inc(s_tabd, 1),
                e.wait_ge(s_tabd, 1),
                e.scalar_tensor_tensor(out=small[:, 2, :], in0=small[:, 1, :], scalar=-float(NE), in1=small[:, 0, :],
                                       op0=ALU.mult, op1=ALU.add).then_inc(s_tabd, 1),
                e.tensor_scalar(small[:, 3, :], page_no, float(NE), None, ALU.is_lt).then_inc(s_tabd, 1),
                e.wait_ge(s_tabd, 3),
                e.tensor_tensor(small[:, 0, :], page_no, small[:, 2, :], ALU.subtract).then_inc(s_tabd, 1),
                e.wait_ge(s_tabd, 4),
                e.tensor_tensor(small[:, 0, :], small[:, 0, :], small[:, 3, :], ALU.mult).then_inc(s_tabd, 1),
                e.wait_ge(s_tabd, 5),
                e.tensor_tensor(small[:, 0, :], small[:, 0, :], small[:, 2, :], ALU.add).then_inc(s_tabd, 1),
                e.wait_ge(s_tabd, 6),
                e.tensor_scalar(table_i[:, :], small[:, 0, :], float(P), float((NE - 1) * P), ALU.mult, ALU.min)
                 .then_inc(s_tabd, 1)]},
            {"sp": lambda e: [
                e.wait_ge(s_tabd, 7),
                e.dma_start(table_d.rearrange("(c p) -> p c", p=P), table_i[:, :],
                            allow_slow_non_contiguous=True).then_inc(s_tab, 16),
                e.wait_ge(s_tab, 32),
                e.dma_start(tab[:, :], table_d.rearrange("(o c) -> o c", o=1)).then_inc(s_tab, 16),
                e.dma_start(page_expert.bitcast(I32), table_d[0:NPAGE].partition_broadcast(P)).then_inc(s_tab, 16),
                e.wait_ge(s_tab, 64),
                e.wait_ge(s_scat, 16 * NT * TOPK * NB)]},
            {"dve": lambda e: [
                e.wait_ge(s_tab, 64),
                e.tensor_copy(page_expert, page_expert.bitcast(I32)).then_inc(s_tabd, 1)]},
        ]

        TX, GT, YP = bank[0:2], bank[2:4], [bank[4:6], bank[6:8]]

        def b_group(k, g):
            return 4 * k + g

        def b_rows(G):
            return pages[bass.ds(G * GRP * P, GRP * P), :].rearrange("(j p) d -> p j d", p=P)

        def b_load(k):
            def f(e):
                _, wrow = nc.values_load_multi_w_load_instructions(
                    tab[0:1, bass.ds(k * 4 * GRP, 4 * GRP)], engines=[mybir.EngineType.SP],
                    min_val=0, max_val=(NE - 1) * P,
                    skip_runtime_bounds_check_because="every entry is a count, at least 0, and cut at the last expert")
                for g in range(4):
                    G = b_group(k, g)
                    wait(e, s_Y, G - 3)
                    own_d.wait(e, "row", G - 4)
                    e.dma_start(x_in[:, g, :, :], b_rows(G)).then_inc(s_xl[g], 16)
                    for j in range(GRP):
                        e.dma_start(w_in[:, g, j, :], wexp[bass.ds(wrow[g * GRP + j], P), :]).then_inc(s_xl[g], 16)
            return {"sp": f}

        def b_scatter(k):
            def f(e):
                for g in range(4):
                    G = b_group(k, g)
                    wait(e, s_YD, G + 1)
                    wait(e, s_YA, G + 1)
                    if g < 3:
                        wait(e, s_ys[g + 1], 16 * GRP * k)
                    else:
                        wait(e, s_ys[0], 16 * GRP * (k + 1))
                    apart(e)
                    for j in range(GRP):
                        e.indirect_dma_start(
                            out=results, in_=y_sb[:, g, j, :], in_offset=None,
                            out_offset=bass.IndirectOffsetOnAxis(ap=res_row[:, g, j:j + 1], axis=0),
                        ).then_inc(s_ys[g], 16)
            return {"pool": f}

        XL = 16 * (GRP + 1)

        def b_steps(k, which):
            steps = []
            for g in which:
                G = b_group(k, g)
                first = isinstance(k, int) and k == 0

                def tr(e, G=G, g=g):
                    e.wait_ge(s_xl[g], XL * (k + 1))
                    wait(e, s_XT, G - 1)
                    for j in range(GRP):
                        last = e.transpose(TX[g % 2][:, j * P:(j + 1) * P], x_in[:, g, j, 0:D], ident)
                    last.then_inc(s_T, 1)

                def xt(e, G=G, g=g):
                    e.wait_ge(s_T, G + 1)
                    wait(e, s_G, G - 1)
                    e.tensor_copy(x_T[g % 2], TX[g % 2][:, :]).then_inc(s_XT, 1)

                def own(e, G=G, g=g, k=k):
                    x_hit = page_expert[:, bass.ds(G * GRP, GRP)].rearrange("p (j o) -> p j o", o=1) \
                        .broadcast_to([P, GRP, TOPK])
                    own_d.wait(e, "row", G - 1)
                    e.wait_ge(s_xl[g], XL * (k + 1))
                    own_d.done(e.tensor_tensor(hit[:, :, :], x_in[:, g, :, IDS:WTS], x_hit, ALU.is_equal), "hit")
                    own_d.wait(e, "hit", G)
                    own_d.done(e.tensor_tensor(
                        hit_k[:, :, :], hit[:, :, :],
                        iota_e[:, 0:TOPK].rearrange("p (o k) -> p o k", o=1).broadcast_to([P, GRP, TOPK]), ALU.mult),
                        "hit_k")
                    own_d.done(e.tensor_tensor(hit_w[:, :, :], hit[:, :, :], x_in[:, g, :, WTS:ROW], ALU.mult), "hit_w")
                    own_d.wait(e, "hit_k", G)
                    own_d.done(e.tensor_reduce(rank_of[:, :], hit_k[:, :, :], AX.X, ALU.add), "rank")
                    own_d.wait(e, "hit_w", G)
                    wait(e, s_YD, G - 3)
                    wait(e, s_YA, G - 3)
                    own_d.done(e.tensor_reduce(w_of[:, g, :], hit_w[:, :, :], AX.X, ALU.add), "w")
                    own_d.wait(e, "rank", G)
                    wait(e, s_ys[g], 16 * GRP * k)
                    own_d.done(e.tensor_tensor(res_row[:, g, :], rank_of[:, :], x_in[:, g, :, BASE], ALU.add), "row")

                def gate(e, G=G - 1, g=(g - 1) % 4):
                    e.wait_ge(s_XT, G + 1)
                    wait(e, s_H, G - 1)
                    for j in range(GRP):
                        half = 64 * (j % 2)
                        last = e.matmul(GT[g % 2][half:half + 64, (j // 2) * P:(j // 2 + 1) * P],
                                        w_in[:, g, j, 0:INTER], x_T[g % 2][:, j * P:(j + 1) * P],
                                        start=True, stop=True)
                    last.then_inc(s_G, 1)

                def silu(e, G=G - 1, g=(g - 1) % 4):
                    e.wait_ge(s_G, G + 1)
                    wait(e, s_Y, G - 1)
                    e.activation(h_g[g % 2], GT[g % 2][:, 0:2 * P], ACT.Silu).then_inc(s_H, 1)

                def down(e, G=G - 2, g=(g - 2) % 4):
                    e.wait_ge(s_H, G + 1)
                    wait(e, s_YD, G - 1)
                    wait(e, s_YA, G - 1)
                    for j in range(GRP):
                        half = 64 * (j % 2)
                        last = e.matmul(YP[g % 2][j % 2][:, (j // 2) * D:(j // 2 + 1) * D],
                                        h_g[g % 2][half:half + 64, (j // 2) * P:(j // 2 + 1) * P],
                                        w_in[half:half + 64, g, j, INTER:WROW], start=True, stop=True)
                    last.then_inc(s_Y, 1)

                def y_out(e, par, s_mine, G=G - 2, g=(g - 2) % 4, stores=k if g >= 2 else k - 1):
                    e.wait_ge(s_Y, G + 1)
                    own_d.wait(e, "w", G)
                    wait(e, s_ys[g], 16 * GRP * stores)
                    for j in range(par, GRP, 2):
                        dst, src = y_sb[:, g, j, :], YP[g % 2][par][:, (j // 2) * D:(j // 2 + 1) * D]
                        if par == 0:
                            last = e.tensor_scalar(dst, src, w_of[:, g, j:j + 1], None, ALU.mult)
                        else:
                            last = e.activation(dst, src, ACT.Identity, scale=w_of[:, g, j:j + 1])
                    last.then_inc(s_mine, 1)
                step = {}
                pe, dve, act = [], [], []
                end = isinstance(k, int) and k == NGRP // 4
                if not end:
                    pe.append(tr)
                    dve += [xt, own]
                if not (first and g < 1) and not (end and g > 0):
                    pe.append(gate)
                    act.append(silu)
                if not (first and g < 2):
                    pe.append(down)
                    dve.append(lambda e, f=y_out: f(e, 0, s_YD))
                    act.append(lambda e, f=y_out: f(e, 1, s_YA))
                for name, fs in (("pe", pe), ("dve", dve), ("act", act)):
                    step[name] = lambda e, fs=fs: [f(e) for f in fs]
                steps.append(step)
            return steps

        y8 = [arena[:, i * NT * TOPK * D:(i + 1) * NT * TOPK * D] for i in range(2)]
        gb_bc = arena[:, 2 * NT * TOPK * D:2 * NT * TOPK * D + NB * D].rearrange("p (n d) -> p n d", d=D)
        total_y = [b[:, :, :, :].rearrange("p a h t -> p (a h t)").bitcast(F32)[:, 0:NT * D] for b in (qe, ke)]
        o_sb = [hT, full]
        hs = att[0:INTER, :]
        s_gbd, s_gbp, s_gba = (sem(n) for n in ("s_gbd", "s_gbp", "s_gba"))
        s_sum, s_tot, s_gated, s_fin, s_shp, s_sha = (
            sem(n) for n in ("s_sum", "s_tot", "s_gated", "s_fin", "s_shp", "s_sha"))
        s_y8 = [sem("s_y8_0"), sem("s_y8_1")]
        s_o = [sem("s_o0"), sem("s_o1")]

        ones_sq = sb("ones_sq", [P, P])
        diag4 = xn2[:, :, :]

        def gates():
            steps = [{"dve": lambda e: [e.memset(ones_sq[:, :], 1.0).then_inc(s_gbd, 1)]}]
            for q in range(4):
                def dg(e, q=q):
                    if q:
                        e.wait_ge(s_gbp, q)
                    for a in range(4):
                        last = e.tensor_scalar(diag4[:, a, :], ident, mod[:, 5, 4 * q + a:4 * q + a + 1], None, ALU.mult)
                    last.then_inc(s_gbd, 1)

                def mm(e, q=q):
                    e.wait_ge(s_gbd, q + 2)
                    e.wait_ge(s_YA, NGRP)
                    if q:
                        e.wait_ge(s_gba, q)
                    e.matmul(bank[7][:, :], ones_sq[:, :], diag4.rearrange("p a d -> p (a d)"),
                             start=True, stop=True).then_inc(s_gbp, 1)

                def take(e, q=q):
                    e.wait_ge(s_gbp, q + 1)
                    e.activation(gb_bc[:, 4 * q:4 * q + 4, :].rearrange("p a d -> p (a d)"), bank[7][:, :],
                                 ACT.Identity).then_inc(s_gba, 1)
                steps.append({"dve": dg, "pe": mm, "act": take})
            return steps

        def shared(n, b):
            def up(e):
                wait(e, s_sha, n - 1)
                e.matmul(bank[2 * b][0:INTER, :], col["wgs"], vh[:, bass.ds(n, 1), :].rearrange("p o t -> p (o t)"),
                         start=True, stop=True).then_inc(s_shp, 1)

            def act(e):
                e.wait_ge(s_shp, 2 * n + 1)
                e.activation(hs, bank[2 * b][0:INTER, :], ACT.Silu).then_inc(s_sha, 1)

            def down(e):
                e.wait_ge(s_sha, n + 1)
                wait(e, s_tot, n - 1)
                for t in range(NT):
                    last = e.matmul(bank[2 * b + 1][:, t * D:(t + 1) * D], hs[:, t * P:(t + 1) * P], wds_sb[:, :],
                                    start=True, stop=True)
                last.then_inc(s_shp, 1)
            return {"pe": lambda e: [up(e), down(e)], "act": act}

        def y8_load(n, b, k):
            def f(e):
                wait(e, s_sum, n - 1)
                e.dma_start(y8[b].rearrange("p (t r) -> p t r", t=NT),
                            results[bass.ds(n * S * TOPK, S * TOPK), :].rearrange("(t p k) d -> p t (k d)", t=NT, p=P)) \
                 .then_inc(s_y8[b], 16)
            return {"sp": f}

        def sums(n, b, k):
            def total_(e):
                e.wait_ge(s_y8[b], 16 * (k + 1))
                wait(e, s_gated, n - 1)
                e.tensor_reduce(total_y[b].rearrange("p (t d) -> p t d", d=D),
                                y8[b].rearrange("p (t k d) -> p t d k", t=NT, k=TOPK), AX.X, ALU.add).then_inc(s_sum, 1)
                e.wait_ge(s_sum, n + 1)
                e.wait_ge(s_shp, 2 * n + 2)
                e.tensor_tensor(total_y[b], total_y[b], bank[2 * b + 1][:, :], ALU.add).then_inc(s_tot, 1)

            def gate(e):
                wait(e, s_tot, n + 1)
                wait(e, s_o[b], 16 * k)
                e.tensor_tensor(o_sb[b].rearrange("p (t d) -> p t d", d=D), total_y[b].rearrange("p (t d) -> p t d", d=D),
                                gb_bc[:, bass.ds(n, 1), :].broadcast_to([P, NT, D]), ALU.mult).then_inc(s_gated, 1)
                wait(e, s_gated, n + 1)
                e.tensor_tensor(o_sb[b].rearrange("p (t d) -> p t d", d=D), o_sb[b].rearrange("p (t d) -> p t d", d=D),
                                seq(n), ALU.add).then_inc(s_fin, 1)

            def put(e):
                wait(e, s_fin, n + 1)
                e.dma_start(out[bass.ds(n, 1)].rearrange("o (t p) d -> (o p) t d", p=P),
                            o_sb[b].rearrange("p (t d) -> p t d", d=D)).then_inc(s_o[b], 16)
            return {"dve": total_, "pool": gate}, {"sp": put}

        def stage_c(e, name):
            if name == "sp":
                for g in range(4):
                    e.wait_ge(s_ys[g], 16 * GRP * NGRP // 4)
                run(name, e, [y8_load(0, 0, 0), y8_load(1, 1, 0)])
            if name == "pool":
                e.wait_ge(s_gba, 4)

            def pair(k, more=True):
                for b in range(2):
                    n = 2 * k + b
                    sum_, put = sums(n, b, k)
                    run(name, e, [shared(n, b), sum_] + ([y8_load(n + 2, b, k + 1)] if more else []) + [put])
            pair(0)
            with e.Fori(1, NB // 2 - 1) as k:
                pair(k)
            pair(NB // 2 - 1, more=False)
            if name == "sp":
                for b in range(2):
                    e.wait_ge(s_o[b], 16 * NB // 2)

        def program(name):
            def f(e):
                run(name, e, setup)
                run(name, e, turn_a(-2, ex_=False, mx_=False, post_=False, scat_=False))
                run(name, e, turn_a(-1, ex_=False, post_=False, scat_=False))
                run(name, e, turn_a(0, post_=False, scat_=False))
                run(name, e, turn_a(1, scat_=False))
                with e.Fori(2, NB - 2) as i:
                    run(name, e, turn_a(i))
                run(name, e, turn_a(NB - 2, pre_=False))
                run(name, e, turn_a(NB - 1, pre_=False, mx_=False))
                run(name, e, merge((post(NB - 1), 0.0, 1.0), (scatters(NB - 2), 0.0, 0.8)))
                run(name, e, scatters(NB - 1))
                run(name, e, table)
                if name == "sp":
                    run(name, e, [b_load(0)])
                    with e.Fori(1, NGRP // 4) as k:
                        run(name, e, [b_load(k)])
                if name == "pool":
                    run(name, e, [b_scatter(0)])
                    with e.Fori(1, NGRP // 4) as k:
                        run(name, e, [b_scatter(k)])
                if name in ("pe", "dve", "act"):
                    if name == "pe":
                        e.wait_ge(s_tabd, 7)
                        post_d.wait(e, "zs1", LAST)
                        pre_d.wait(e, "v", LAST)
                    if name in ("dve", "act"):
                        e.wait_ge(s_tabd, 8)
                    run(name, e, b_steps(0, range(4)))
                    with e.Fori(1, NGRP // 4) as k:
                        run(name, e, b_steps(k, range(4)))
                    run(name, e, b_steps(NGRP // 4, range(2)))
                run(name, e, gates())
                stage_c(e, name)
            return f

        block = ctx.enter_context(nc.Block())
        block.sync(program("sp"))
        block.gpsimd(program("pool"))
        block.tensor(program("pe"))
        block.vector(program("dve"))
        block.scalar(program("act"))


def kernel(L0_attn_x, L0_attn_qkv_w, L0_attn_qkv_b, L0_attn_proj_w, L0_attn_proj_b, L0_ffn_router_w,
           L0_ffn_expert_bias, L0_ffn_w_gate, L0_ffn_w_down, L0_ffn_w_gate_shared, L0_ffn_w_down_shared,
           L0_c, L0_wmod):
    import ml_dtypes
    import numpy as np
    import concourse.bacc as bacc
    from concourse.bass_utils import run_bass_kernel_spmd

    a = lambda v: np.asarray(v)
    qkv_w, qkv_b = a(L0_attn_qkv_w), a(L0_attn_qkv_b)
    h2, par, d = np.arange(8), np.arange(2), np.arange(HD)
    order = ((2 * h2[None, None, :] + par[:, None, None]) * HD + d[None, :, None]).reshape(-1)
    turned = ((2 * h2[None, None, :] + par[:, None, None]) * HD + ((d + HD // 2) % HD)[None, :, None]).reshape(-1)
    wq, wk, wv = qkv_w[0:D], qkv_w[D:2 * D], qkv_w[2 * D:3 * D]
    bq, bk, bv = qkv_b[0:D], qkv_b[D:2 * D], qkv_b[2 * D:3 * D]
    wts = np.concatenate([
        wq[order].T, wq[turned].T, wk[order].T, wk[turned].T, wv.T, a(L0_attn_proj_w).T, a(L0_ffn_router_w).T,
        a(L0_wmod), a(L0_c).T, a(L0_ffn_w_gate_shared).T, bq[order][:, None], bq[turned][:, None],
        bk[order][:, None], bk[turned][:, None], a(L0_attn_proj_b)[:, None]], axis=1)
    wg, wd = a(L0_ffn_w_gate).transpose(0, 2, 1), a(L0_ffn_w_down).transpose(0, 2, 1)
    wexp = np.concatenate([wg, np.concatenate([wd, wd], axis=1)], axis=2).reshape(NE * P, WROW)

    freqs = (1.0 / 10000.0 ** (np.arange(HD // 2, dtype=np.float32) / np.float32(HD // 2))).astype(np.float32)
    angle = np.arange(S, dtype=np.float32)[:, None] * freqs[None, :]
    dd = order % HD
    cos = np.cos(angle).astype(np.float32).T[dd % (HD // 2)]
    sin = np.sin(angle).astype(np.float32).T[dd % (HD // 2)] * np.where(dd < HD // 2, -1.0, 1.0)[:, None]
    page_no = np.arange(PCOL)[None, :] * P + np.arange(P)[:, None]
    row_0 = (np.arange(NT)[None, :] * P + np.arange(P)[:, None]) * TOPK
    row_free = NB * S * TOPK + np.arange(GRP * P).reshape(P, GRP)
    const = np.concatenate([cos, sin, np.eye(P), np.tile(np.arange(NE), (P, 1)), page_no, row_0, row_free],
                           axis=1).astype(np.float32)
    r, c = np.arange(P)[:, None], np.arange(P)[None, :]
    constb = np.concatenate([np.where(c > r, -1e9, 0.0), np.where(r > c, -1e9, 0.0), np.eye(P), (r < c) + TAKEN * (r == c),
                             np.ones((P, P))], axis=1).astype(ml_dtypes.bfloat16)
    arrays = {"x": a(L0_attn_x), "wts": wts, "bvec": bv, "brow": a(L0_ffn_expert_bias)[None, :],
              "wexp": wexp, "wds": a(L0_ffn_w_down_shared).T, "const": const, "constb": constb}
    arrays = {k: np.ascontiguousarray(v) for k, v in arrays.items()}
    nc = bacc.Bacc("TRN2", target_bir_lowering=False, num_devices=1)
    ins = [nc.dram_tensor(k, v.shape, mybir.dt.from_np(v.dtype), kind="ExternalInput").ap()
           for k, v in arrays.items()]
    out = nc.dram_tensor("out", (NB, S, D), F32, kind="ExternalOutput").ap()
    build(nc, *ins, out)
    return run_bass_kernel_spmd(nc, [arrays], core_ids=[0]).results[0]["out"]
```
